# Optimizing a Trainium2 kernel written in Bass

```python
import numpy as np
import jax
import jax.numpy as jnp

def _softmax(x, axis=-1):
    return jax.nn.softmax(x, axis=axis)

def _gelu(x):
    return jax.nn.gelu(x, approximate=True)

def _silu(x):
    return jax.nn.silu(x)

def _sigmoid(x):
    return jax.nn.sigmoid(x)

def _layernorm(x, axis=-1, eps=1e-05):
    m = jnp.mean(x, axis=axis, keepdims=True)
    v = jnp.var(x, axis=axis, keepdims=True)
    return (x - m) / jnp.sqrt(v + eps)

def _scatter_add(tgt, idx, src, axis=0):
    return tgt.at[idx].add(src)

def _segment_sum(src, seg, n):
    return jax.ops.segment_sum(src, seg, n)
kernel_name = 'mk_xattn_seq_d2_seqx_r8_3a53a0'

def setup_inputs(seed: int=0):
    np.random.seed(seed)
    _w = jnp.asarray

    def _rec_inputs():
        import jax
        import jax.numpy as jnp
        _rk = jax.random.key(seed)
        x = 7.22e-05 + 1 * jax.random.normal(jax.random.fold_in(_rk, 1), (16, 128, 128), jnp.float32)
        _lenS = 128 - jax.random.randint(jax.random.fold_in(_rk, 7), (16,), 0, max(1, 128 // 4) + 1, jnp.int32)
        _lenS2 = 128 - jax.random.randint(jax.random.fold_in(_rk, 8), (16,), 0, max(1, 128 // 4) + 1, jnp.int32)
        _ctx_1024P = jax.random.normal(jax.random.fold_in(_rk, 11), (16, 16, 128), jnp.float32)
        _ctx_1024c = jax.random.dirichlet(jax.random.fold_in(_rk, 511), 0.3 * jnp.ones((16,), jnp.float32), (16, 128))
        _ctx_1024t = jnp.einsum('bsk,bkd->bsd', _ctx_1024c, _ctx_1024P)
        _ctx_1024t = _ctx_1024t * jax.lax.rsqrt(jnp.mean(jnp.square(_ctx_1024t)) + 1e-12) * 0.953939
        ctx_1024 = 4.13588e-05 + 0.999923 * (_ctx_1024t + 0.3 * jax.random.normal(jax.random.fold_in(_rk, 611), (16, 128, 128), jnp.float32))
        _validS = jnp.arange(128)[None, :] < _lenS[:, None]
        _validS2 = jnp.arange(128)[None, :] < _lenS2[:, None]
        _causal = jnp.tril(jnp.ones((128, 128), dtype=bool))
        mask_BxSxS2_fk0 = jnp.where(jnp.broadcast_to(_validS2[:, None, :], (16, 128, 128)), 0.0, 1.0).astype(jnp.float32)
        return (x, ctx_1024, mask_BxSxS2_fk0)
    x, ctx_1024, mask_BxSxS2_fk0 = _rec_inputs()

    def _L0_xattn_setup():
        import jax, jax.numpy as jnp
        import numpy as np
        import math
        B, S, D, H, FF = (4, 256, 128, 16, 512)
        HD = D // H
        EPS = 1e-05

        def _layer_norm(x, g, b):
            m = jnp.mean(x, axis=-1, keepdims=True)
            v = jnp.mean((x - m) ** 2, axis=-1, keepdims=True)
            return (x - m) * jax.lax.rsqrt(v + EPS) * g + b

        def _self_attn(x, mask, Wq, bq, Wk, bk, Wv, bv, Wo, bo):
            b, s, d = x.shape
            q = (x @ Wq.T + bq).reshape(b, s, H, HD)
            k = (x @ Wk.T + bk).reshape(b, s, H, HD)
            v = (x @ Wv.T + bv).reshape(b, s, H, HD)
            score = jnp.einsum('bshd,bthd->bhst', q, k) / math.sqrt(HD)
            score = score + (1.0 - mask[:, None, :, :]) * -1000000000.0
            p = jax.nn.softmax(score, axis=-1)
            o = jnp.einsum('bhst,bthd->bshd', p, v).reshape(b, s, d)
            return o @ Wo.T + bo
        key = jax.random.key(seed)
        ks = jax.random.split(key, 16)
        sd = 0.02
        inp = {'tgt': jax.random.normal(ks[0], (B, S, D), jnp.float32), 'memory': jax.random.normal(ks[1], (B, S, D), jnp.float32), 'mask': jnp.broadcast_to(jnp.tril(jnp.ones((S, S), jnp.float32)), (B, S, S)), 'Wq': jax.random.normal(ks[2], (D, D), jnp.float32) * sd, 'bq': jnp.zeros((D,), jnp.float32), 'Wk': jax.random.normal(ks[3], (D, D), jnp.float32) * sd, 'bk': jnp.zeros((D,), jnp.float32), 'Wv': jax.random.normal(ks[4], (D, D), jnp.float32) * sd, 'bv': jnp.zeros((D,), jnp.float32), 'Wo': jax.random.normal(ks[5], (D, D), jnp.float32) * sd, 'bo': jnp.zeros((D,), jnp.float32), 'Wg': jax.random.normal(ks[6], (D, D), jnp.float32) * sd, 'bg': jnp.zeros((D,), jnp.float32), 'W1': jax.random.normal(ks[7], (FF, D), jnp.float32) * sd, 'b1': jnp.zeros((FF,), jnp.float32), 'W2': jax.random.normal(ks[8], (D, FF), jnp.float32) * sd, 'b2': jnp.zeros((D,), jnp.float32), 'g1': jnp.ones((D,), jnp.float32), 'be1': jnp.zeros((D,), jnp.float32), 'g2': jnp.ones((D,), jnp.float32), 'be2': jnp.zeros((D,), jnp.float32)}
        return inp
    _L0_xattn_all = _L0_xattn_setup()
    _L0_xattn_in = {k: v for k, v in _L0_xattn_all.items() if k in ('Wq', 'bq', 'Wk', 'bk', 'Wv', 'bv', 'Wo', 'bo', 'Wg', 'bg', 'W1', 'b1', 'W2', 'b2', 'g1', 'be1', 'g2', 'be2')}
    del _L0_xattn_all

    def _L1_xattn_setup():
        import jax, jax.numpy as jnp
        import numpy as np
        D_MODEL = 128
        N_HEADS = 16
        D_K = D_MODEL // N_HEADS
        LN_EPS = 1e-05

        def _attention(query, key_value, W_qkv, b_qkv, W_o, b_o, ln_gamma, ln_beta):
            B, Sq, _ = query.shape
            Skv = key_value.shape[1]
            Wq, Wk, Wv = (W_qkv[:D_MODEL], W_qkv[D_MODEL:2 * D_MODEL], W_qkv[2 * D_MODEL:])
            bq, bk, bv = (b_qkv[:D_MODEL], b_qkv[D_MODEL:2 * D_MODEL], b_qkv[2 * D_MODEL:])
            Q = (query @ Wq.T + bq).reshape(B, Sq, N_HEADS, D_K).transpose(0, 2, 1, 3)
            K = (key_value @ Wk.T + bk).reshape(B, Skv, N_HEADS, D_K).transpose(0, 2, 1, 3)
            V = (key_value @ Wv.T + bv).reshape(B, Skv, N_HEADS, D_K).transpose(0, 2, 1, 3)
            scores = jnp.einsum('bhqd,bhkd->bhqk', Q.astype(jnp.float32), K.astype(jnp.float32))
            scores = scores / np.sqrt(D_K)
            attn = jax.nn.softmax(scores, axis=-1)
            context = jnp.einsum('bhqk,bhkd->bhqd', attn, V.astype(jnp.float32)).astype(query.dtype)
            context = context.transpose(0, 2, 1, 3).reshape(B, Sq, D_MODEL)
            output = context @ W_o.T + b_o
            x = output + query
            mu = jnp.mean(x, axis=-1, keepdims=True)
            var = jnp.mean(jnp.square(x - mu), axis=-1, keepdims=True)
            return (x - mu) / jnp.sqrt(var + LN_EPS) * ln_gamma + ln_beta
        key = jax.random.key(seed)
        ks = jax.random.split(key, 8)
        B, Sq, Skv = (2, 256, 256)
        scale = 1.0 / np.sqrt(D_MODEL)
        return {'query': jax.random.normal(ks[0], (B, Sq, D_MODEL), dtype=jnp.float32), 'key_value': jax.random.normal(ks[1], (B, Skv, D_MODEL), dtype=jnp.float32), 'W_qkv': jax.random.normal(ks[2], (3 * D_MODEL, D_MODEL), dtype=jnp.float32) * scale, 'b_qkv': jax.random.normal(ks[3], (3 * D_MODEL,), dtype=jnp.float32) * 0.01, 'W_o': jax.random.normal(ks[4], (D_MODEL, D_MODEL), dtype=jnp.float32) * scale, 'b_o': jax.random.normal(ks[5], (D_MODEL,), dtype=jnp.float32) * 0.01, 'ln_gamma': jnp.ones((D_MODEL,), dtype=jnp.float32), 'ln_beta': jnp.zeros((D_MODEL,), dtype=jnp.float32)}
    _L1_xattn_all = _L1_xattn_setup()
    _L1_xattn_in = {k: v for k, v in _L1_xattn_all.items() if k in ('W_qkv', 'b_qkv', 'W_o', 'b_o', 'ln_gamma', 'ln_beta')}
    del _L1_xattn_all
    return {'x': x, 'ctx_1024': ctx_1024, 'mask_BxSxS2_fk0': mask_BxSxS2_fk0, 'L0_xattn_Wq': _L0_xattn_in['Wq'], 'L0_xattn_bq': _L0_xattn_in['bq'], 'L0_xattn_Wk': _L0_xattn_in['Wk'], 'L0_xattn_bk': _L0_xattn_in['bk'], 'L0_xattn_Wv': _L0_xattn_in['Wv'], 'L0_xattn_bv': _L0_xattn_in['bv'], 'L0_xattn_Wo': _L0_xattn_in['Wo'], 'L0_xattn_bo': _L0_xattn_in['bo'], 'L0_xattn_Wg': _L0_xattn_in['Wg'], 'L0_xattn_bg': _L0_xattn_in['bg'], 'L0_xattn_W1': _L0_xattn_in['W1'], 'L0_xattn_b1': _L0_xattn_in['b1'], 'L0_xattn_W2': _L0_xattn_in['W2'], 'L0_xattn_b2': _L0_xattn_in['b2'], 'L0_xattn_g1': _L0_xattn_in['g1'], 'L0_xattn_be1': _L0_xattn_in['be1'], 'L0_xattn_g2': _L0_xattn_in['g2'], 'L0_xattn_be2': _L0_xattn_in['be2'], 'L1_xattn_W_qkv': _L1_xattn_in['W_qkv'], 'L1_xattn_b_qkv': _L1_xattn_in['b_qkv'], 'L1_xattn_W_o': _L1_xattn_in['W_o'], 'L1_xattn_b_o': _L1_xattn_in['b_o'], 'L1_xattn_ln_gamma': _L1_xattn_in['ln_gamma'], 'L1_xattn_ln_beta': _L1_xattn_in['ln_beta']}

def reference(x, ctx_1024, mask_BxSxS2_fk0, L0_xattn_Wq, L0_xattn_bq, L0_xattn_Wk, L0_xattn_bk, L0_xattn_Wv, L0_xattn_bv, L0_xattn_Wo, L0_xattn_bo, L0_xattn_Wg, L0_xattn_bg, L0_xattn_W1, L0_xattn_b1, L0_xattn_W2, L0_xattn_b2, L0_xattn_g1, L0_xattn_be1, L0_xattn_g2, L0_xattn_be2, L1_xattn_W_qkv, L1_xattn_b_qkv, L1_xattn_W_o, L1_xattn_b_o, L1_xattn_ln_gamma, L1_xattn_ln_beta):
    import jax
    import jax.numpy as jnp

    def _L0_xattn_ref(tgt, memory, mask, Wq, bq, Wk, bk, Wv, bv, Wo, bo, Wg, bg, W1, b1, W2, b2, g1, be1, g2, be2):
        import jax, jax.numpy as jnp
        import numpy as np
        import math
        B, S, D, H, FF = (4, 256, 128, 16, 512)
        HD = D // H
        EPS = 1e-05

        def _layer_norm(x, g, b):
            m = jnp.mean(x, axis=-1, keepdims=True)
            v = jnp.mean((x - m) ** 2, axis=-1, keepdims=True)
            return (x - m) * jax.lax.rsqrt(v + EPS) * g + b

        def _self_attn(x, mask, Wq, bq, Wk, bk, Wv, bv, Wo, bo):
            b, s, d = x.shape
            q = (x @ Wq.T + bq).reshape(b, s, H, HD)
            k = (x @ Wk.T + bk).reshape(b, s, H, HD)
            v = (x @ Wv.T + bv).reshape(b, s, H, HD)
            score = jnp.einsum('bshd,bthd->bhst', q, k) / math.sqrt(HD)
            score = score + (1.0 - mask[:, None, :, :]) * -1000000000.0
            p = jax.nn.softmax(score, axis=-1)
            o = jnp.einsum('bhst,bthd->bshd', p, v).reshape(b, s, d)
            return o @ Wo.T + bo
        tgt1 = _layer_norm(tgt, g1, be1)
        tgt = tgt + _self_attn(tgt1, mask, Wq, bq, Wk, bk, Wv, bv, Wo, bo)
        tgt = tgt + (memory @ Wg.T + bg)
        tgt1 = _layer_norm(tgt, g2, be2)
        ff = jax.nn.relu(tgt1 @ W1.T + b1) @ W2.T + b2
        return tgt + ff

    def _L1_xattn_ref(query, key_value, W_qkv, b_qkv, W_o, b_o, ln_gamma, ln_beta):
        import jax, jax.numpy as jnp
        import numpy as np
        D_MODEL = 128
        N_HEADS = 16
        D_K = D_MODEL // N_HEADS
        LN_EPS = 1e-05

        def _attention(query, key_value, W_qkv, b_qkv, W_o, b_o, ln_gamma, ln_beta):
            B, Sq, _ = query.shape
            Skv = key_value.shape[1]
            Wq, Wk, Wv = (W_qkv[:D_MODEL], W_qkv[D_MODEL:2 * D_MODEL], W_qkv[2 * D_MODEL:])
            bq, bk, bv = (b_qkv[:D_MODEL], b_qkv[D_MODEL:2 * D_MODEL], b_qkv[2 * D_MODEL:])
            Q = (query @ Wq.T + bq).reshape(B, Sq, N_HEADS, D_K).transpose(0, 2, 1, 3)
            K = (key_value @ Wk.T + bk).reshape(B, Skv, N_HEADS, D_K).transpose(0, 2, 1, 3)
            V = (key_value @ Wv.T + bv).reshape(B, Skv, N_HEADS, D_K).transpose(0, 2, 1, 3)
            scores = jnp.einsum('bhqd,bhkd->bhqk', Q.astype(jnp.float32), K.astype(jnp.float32))
            scores = scores / np.sqrt(D_K)
            attn = jax.nn.softmax(scores, axis=-1)
            context = jnp.einsum('bhqk,bhkd->bhqd', attn, V.astype(jnp.float32)).astype(query.dtype)
            context = context.transpose(0, 2, 1, 3).reshape(B, Sq, D_MODEL)
            output = context @ W_o.T + b_o
            x = output + query
            mu = jnp.mean(x, axis=-1, keepdims=True)
            var = jnp.mean(jnp.square(x - mu), axis=-1, keepdims=True)
            return (x - mu) / jnp.sqrt(var + LN_EPS) * ln_gamma + ln_beta
        return _attention(query, key_value, W_qkv, b_qkv, W_o, b_o, ln_gamma, ln_beta)
    x = _L0_xattn_ref(x, ctx_1024, mask_BxSxS2_fk0, L0_xattn_Wq, L0_xattn_bq, L0_xattn_Wk, L0_xattn_bk, L0_xattn_Wv, L0_xattn_bv, L0_xattn_Wo, L0_xattn_bo, L0_xattn_Wg, L0_xattn_bg, L0_xattn_W1, L0_xattn_b1, L0_xattn_W2, L0_xattn_b2, L0_xattn_g1, L0_xattn_be1, L0_xattn_g2, L0_xattn_be2)
    x = _L1_xattn_ref(x, ctx_1024, L1_xattn_W_qkv, L1_xattn_b_qkv, L1_xattn_W_o, L1_xattn_b_o, L1_xattn_ln_gamma, L1_xattn_ln_beta)
    return x

_drawn_inputs = setup_inputs


def setup_inputs(seed=0):
    import zlib

    import numpy as np

    out = dict(_drawn_inputs(seed))
    spreads = {'L0_xattn_bq': (0.0, 0.8),
     'L0_xattn_bk': (0.0, 0.8),
     'L0_xattn_bv': (0.0, 0.424),
     'L0_xattn_bo': (0.0, 0.1),
     'L0_xattn_bg': (0.0, 0.1),
     'L0_xattn_b1': (0.0, 0.337),
     'L0_xattn_b2': (0.0, 0.1),
     'L0_xattn_g1': (1.0, 0.6),
     'L0_xattn_be1': (0.0, 0.8),
     'L0_xattn_g2': (1.0, 0.6),
     'L0_xattn_be2': (0.0, 0.8),
     'L1_xattn_ln_gamma': (1.0, 0.2),
     'L1_xattn_ln_beta': (0.0, 0.1)}
    factors = {'L0_xattn_Wq': 8.0,
     'L0_xattn_Wk': 8.0,
     'L0_xattn_Wv': 3.026,
     'L1_xattn_b_qkv': 7.969,
     'L1_xattn_b_o': 5.785}
    for name, (base, spread) in spreads.items():
        noise = np.random.default_rng([zlib.crc32(name.encode()), seed]).standard_normal(out[name].shape)
        drawn = base * np.exp(spread * noise) if base else spread * noise
        out[name] = jnp.asarray(drawn.astype(out[name].dtype))
    for name, factor in factors.items():
        out[name] = (out[name] * factor).astype(out[name].dtype)
    return out
```

```python
import concourse.bass as bass
from concourse import mybir
from contextlib import ExitStack

F32 = mybir.dt.float32
BF16 = mybir.dt.bfloat16
ALU = mybir.AluOpType
ACT = mybir.ActivationFunctionType

NB, S, D = 16, 128, 128
NH, HD, FF = 16, 8, 512
GB = 2
NG = NB // GB
TG = GB * S
UH = 4
UB = NH // UH
NU = GB * UB
NJ = FF // 128
NP = 3
NSLOT = 6
KR = NSLOT * HD
VW = 32
SCALE = HD ** -0.5
EPS = 1e-5
BIG = 1.0e9
LT, LP = 2, 4
RT, RP = 4, 4
WROTE = 16 * 3 * GB

BQ, BK, BV, G1, BE1, G2, BE2, B1, BQ1, BK1, BV1 = 0, 1, 2, 3, 4, 5, 6, 7, 11, 12, 13
NVEC = 14
R_BO, R_BG, R_B2, R_BO1, R_GAM, R_BET, NREP = 0, 1, 2, 3, 4, 5, 6
W_Q, W_K, W_V, W_O, W_G, W_1, W_2, W_Q1, W_K1, W_V1, W_O1, NW = 0, 1, 2, 3, 4, 5, 9, 13, 14, 15, 16, 17


def build(nc, x, ctx_, mask, Wq, bq, Wk, bk, Wv, bv, Wo, bo, Wg, bg, W1, b1, W2, b2, g1, be1, g2, be2,
          Wqkv1, bqkv1, Wo1, bo1, gam, bet, out):
    x_v = x.rearrange("(g b) s d -> g s b d", b=GB)
    c_v = ctx_.rearrange("(g b) s d -> g s b d", b=GB)
    o_v = out.rearrange("(g b) s d -> g s b d", b=GB)
    row = lambda a: a.rearrange("(r n) -> r n", n=128)

    scr = {k: nc.dram_tensor(f"stack_{k}", [2 * NG, GB, NSLOT, 128, S], BF16, kind="Internal").ap()
           for k in "qk"}

    with ExitStack() as es:
        sb = lambda name, shape, dt=F32: es.enter_context(nc.sbuf_tensor(name, shape, dt))
        ps = lambda name: es.enter_context(nc.psum_tensor(name, [128, 512], F32))

        def above_zero(count):
            return not isinstance(count, int) or count > 0

        def settled(eng, i):
            if not isinstance(i, int):
                eng.sem_inc(s_settled[eng.engine.name], 1)

        sem = lambda name: es.enter_context(nc.semaphore(name))
        s_weights, s_vec_rows, s_rep = sem("weights_loaded"), sem("vec_rows_loaded"), sem("rep_loaded")
        s_ident, s_zeroed, s_ones = sem("ident_made"), sem("stacks_zeroed"), sem("ones_set")
        s_rows_p, s_vec_T, s_vecs = sem("rows_permuted"), sem("vectors_turned"), sem("vectors_in_sbuf")
        s_w_T, s_w_sb, s_bias_og = sem("weights_turned"), sem("weights_in_sbuf"), sem("bias_og_made")
        s_x_in, s_c_in, s_stored = sem("x_loaded"), sem("context_loaded"), sem("y_stored")
        s_m_in = [sem(f"mask_loaded{b}") for b in range(GB)]
        s_scores, s_masked, s_shifted = sem("scores_ready"), sem("masked_and_max"), sem("max_subtracted")
        s_turned, s_exps, s_values = sem("scores_turned"), sem("exps_ready"), sem("values_summed")
        s_o_out, s_o_turned, s_rden = sem("o_in_sbuf"), sem("o_turned"), sem("sums_inverted")
        s_o_n, s_o_back, s_aT, s_v_aug = sem("o_normalised"), sem("o_turned_back"), sem("aT_in_sbuf"), sem("v_in_place")
        s_mbias = [sem(f"mask_bias{b}") for b in range(GB)]
        s_stack = [sem(f"stack_read{b}") for b in range(GB)]
        by_kind = lambda name: {k: sem(f"{name}_{k}") for k in ("q0", "k0", "k1", "q1")}
        s_first, s_resid, s_part2 = by_kind("split1"), by_kind("resid"), by_kind("split2")
        s_part3, s_wrote = by_kind("split3"), by_kind("stack_written")
        by_norm = lambda name: {k: sem(f"{name}_{k}") for k in "ab"}
        s_ln, s_ve, s_rstd = by_norm("norm_stats"), by_norm("norm_var"), by_norm("norm_rstd")
        s_P1_ready, s_P1_out = sem("P1_ready"), sem("P1_out")
        s_QK_ready, s_V_ready, s_V_out = sem("QK_ready"), sem("V_ready"), sem("V_out")
        s_k1_ready, s_q1_ready, s_G_ready = sem("K1_ready"), sem("Q1_ready"), sem("G_ready")
        s_R2_ready, s_R2_out = sem("R2_ready"), sem("R2_out")
        s_R3a_ready, s_R3a_out = sem("R3a_ready"), sem("R3a_out")
        s_R3b_ready, s_R3b_out = sem("R3b_ready"), sem("R3b_out")
        s_R4_ready, s_R5_ready, s_R5_out = sem("R4_ready"), sem("R5_ready"), sem("R5_out")
        s_OP_ready, s_OP_out = sem("OP_ready"), sem("OP_out")
        s_xn, s_xb, s_xg, s_xn2 = sem("xn_made"), sem("xb_made"), sem("xg_made"), sem("xn2_made")
        s_x2b, s_x3, s_x3b, s_yg, s_y_out = sem("x2b_made"), sem("x3_made"), sem("x3b_made"), sem("yg_made"), sem("y_made")
        s_settled = {e: sem(f"settled_{e}") for e in ("SP", "DVE", "Pool")}

        ident = sb("ident", [128, 128])
        wraw = sb("wraw", [128, NW * 128])
        wT = sb("wT", [128, NW * 128])
        vec_rows = sb("vec_rows", [NVEC, 128])
        vec_rows_p = sb("vec_rows_p", [NVEC, 128])
        vec = sb("vec", [128, NVEC])
        vec_p = sb("vec_p", [128, NVEC])
        vec_ps = sb("vec_ps", [128, NVEC])
        rep = sb("rep", [128, NREP, 128])
        bias_og = sb("bias_og", [128, 128])
        expo = sb("expo", [128, GB])
        W = lambda n, k=1: wT[:, n * 128:(n + k) * 128]
        x_in = sb("x_in", [128, GB, D])
        c_in = sb("c_in", [128, GB, D])
        m_in = sb("m_in", [128, GB, S])
        mbias = sb("mbias", [128, GB, S])
        xg_all = sb("xg_all", [128, NG * TG])
        x3b_all = sb("x3b_all", [128, NG * TG])
        v_all = sb("v_all", [128, 2 * NG * TG])
        xn = sb("xn", [128, GB, D])
        xb = sb("xb", [128, TG])
        tT = sb("tT", [128, TG])
        cT = sb("cT", [128, TG])
        kinds = ("q0", "k0", "k1", "q1")
        full = {k: sb(f"full_{k}", [128, TG]) for k in kinds}
        resid = {k: sb(f"resid_{k}", [128, TG]) for k in kinds}
        parts = {k: sb(f"parts_{k}", [128, NP, TG], BF16) for k in kinds}
        q_st = sb("q_st", [128, GB, NH, S], BF16)
        k_st = sb("k_st", [128, GB, NH, S], BF16)
        v_aug = sb("v_aug", [128, GB, NH, VW])
        t_sb = sb("t_sb", [128, RT, UH, S])
        mx = sb("mx", [128, RT, UH])
        p_sb = sb("p_sb", [128, RP, UH * S])
        oT_aug = sb("oT_aug", [128, 512])
        rden = sb("rden", [128, NH])
        o_n = sb("o_n", [128, NH, HD])
        aT = sb("aT", [128, GB, S])
        stats = {k: sb(f"stats_{k}", [128, GB, 6]) for k in "ab"}
        mv = {k: sb(f"mv_{k}", [128, GB, 2]) for k in "ab"}
        ve = {k: sb(f"ve_{k}", [128, GB]) for k in "ab"}
        rstd = {k: sb(f"rstd_{k}", [128, GB]) for k in "ab"}
        x2 = sb("x2", [128, TG])
        x2b = sb("x2b", [128, TG])
        xn2 = sb("xn2", [128, GB, D])
        t2T = sb("t2T", [128, TG])
        hT = sb("hT", [128, NJ, TG])
        x3 = sb("x3", [128, TG])
        x3T = sb("x3T", [128, TG])
        yg = sb("yg", [128, GB, D])
        y_out = sb("y_out", [128, GB, D])

        S_ps = [ps("S0"), ps("S1")]
        E_ps = [ps("E0"), ps("E1")]
        O_ps = ps("O")
        N_ps = ps("N")
        D_ps = [ps("D0"), ps("D1")]
        BANK = {"R2": 0, "R3a": 0, "QK": 0, "V": 0, "R5": 0, "G": 0,
                "R3b": 1, "P1": 1, "R4": 1, "K1": 1, "OP": 1, "Q1": 1}
        BANK = {job: D_ps[n] for job, n in BANK.items()}
        wbanks = [D_ps[0], D_ps[1], S_ps[0], S_ps[1], O_ps]

        block = es.enter_context(nc.Block())

        def schedule(eng, body):
            body(-1, None, None, True, False)
            body(0, 0, None, True, False)
            body(1, 0, 0, True, False)
            body(2, 0, 0, True, True)
            with eng.Fori(3, NG - 1) as i:
                body(i, 0, 0, True, True)
            body(NG - 1, 0, 0, False, True)
            body(NG, 1, 0, False, True)
            body(NG + 1, 1, 1, False, True)
            with eng.Fori(NG + 2, 2 * NG) as i:
                body(i, 1, 1, False, False)
            body(2 * NG, None, 1, False, False)

        flat = lambda t: t[:, :, :].rearrange("p b d -> p (b d)")

        @block.sync
        def _(sp):
            def stack_write(kind, buf, grp, at):
                sp.wait_ge(s_part3[kind], grp + 1)
                settled(sp, grp + 1)
                pv = parts[kind][:, :, :].rearrange("p t (b n) -> p t b n", b=GB)
                for n, (first, k) in enumerate(((0, 3), (3, 2), (5, 1))):
                    for b in range(GB):
                        src = pv[:, 0:k, b] if buf == "q" else pv[:, n:n + 1, b].to_broadcast([128, k, S])
                        sp.dma_start(scr[buf][at, b, first:first + k].rearrange("t p n -> p t n"),
                                     src).then_inc(s_wrote[kind], 16)

            def stack_read(i, b, kq, kk, grp):
                sp.wait_ge(s_wrote[kq], WROTE * (grp + 1))
                settled(sp, WROTE * (grp + 1))
                sp.wait_ge(s_wrote[kk], WROTE * (grp + 1))
                settled(sp, WROTE * (grp + 1))
                if above_zero(NU * (i - 1) + UB * (b + 1)):
                    sp.wait_ge(s_scores, NU * (i - 1) + UB * (b + 1))
                settled(sp, NU * (i - 1) + UB * (b + 1))
                for buf, t in (("q", q_st), ("k", k_st)):
                    sp.dma_start(t[0:KR, b].rearrange("p h n -> p (h n)"),
                                 scr[buf][i, b].rearrange("t (d h) n -> (t d) (h n)", h=NH)
                                 ).then_inc(s_stack[b], 16)

            sp.dma_start(x_in[:], x_v[0]).then_inc(s_x_in, 16)
            sp.dma_start(c_in[:], c_v[0]).then_inc(s_c_in, 16)
            for w, n, k in ((Wq, W_Q, 1), (Wk, W_K, 1), (Wv, W_V, 1), (Wg, W_G, 1), (Wqkv1, W_Q1, 3), (Wo, W_O, 1),
                            (W1, W_1, NJ), (Wo1, W_O1, 1)):
                dst = wraw[:, n * 128:(n + k) * 128].rearrange("p (j n) -> p j n", j=k)
                sp.dma_start(dst, w.rearrange("(j p) n -> p j n", p=128)).then_inc(s_weights, 16)
            sp.dma_start(wraw[:, W_2 * 128:(W_2 + NJ) * 128], W2).then_inc(s_weights, 16)
            sp.dma_start(m_in[:, 0], mask[0]).then_inc(s_m_in[0], 16)
            sp.dma_start(m_in[:, 1], mask[1]).then_inc(s_m_in[1], 16)
            sp.wait_ge(s_zeroed, 2)
            settled(sp, 2)

            def inputs(i):
                sp.wait_ge(s_xb, i)
                settled(sp, i)
                sp.wait_ge(s_xn, i)
                settled(sp, i)
                sp.dma_start(x_in[:], x_v[i]).then_inc(s_x_in, 16)
                sp.wait_ge(s_P1_ready, i)
                settled(sp, i)
                sp.dma_start(c_in[:], c_v[i]).then_inc(s_c_in, 16)

            def masks(i):
                for b in range(GB):
                    sp.wait_ge(s_mbias[b], i)
                    settled(sp, i)
                    sp.dma_start(m_in[:, b], mask[GB * i + b]).then_inc(s_m_in[b], 16)

            def store(g):
                sp.wait_ge(s_y_out, g + 1)
                settled(sp, g + 1)
                sp.dma_start(o_v[g], y_out[:]).then_inc(s_stored, 16)

            def body0(i, pre, l2, more):
                if pre and not (isinstance(i, int) and i < 0):
                    masks(i + 1)
                if more:
                    inputs(i + 2)
                if pre:
                    stack_write("k0", "k", i + 1, i + 1)
                    stack_write("q0", "q", i + 1, i + 1)
                    for b in range(GB):
                        stack_read(i + 1, b, "q0", "k0", i + 1)
                    stack_write("k1", "k", i + 1, i + 1 + NG)
                else:
                    for b in range(GB):
                        stack_read(i + 1, b, "q1", "k1", i + 1 - NG)
                if l2:
                    stack_write("q1", "q", i - 2, i - 2 + NG)

            def body1(i):
                for b in range(GB):
                    stack_read(i + 1, b, "q1", "k1", i + 1 - NG)

            body0(-1, True, False, True)
            body0(0, True, False, True)
            body0(1, True, False, True)
            body0(2, True, True, True)
            with sp.Fori(3, NG - 2) as i:
                body0(i, True, True, True)
            body0(NG - 2, True, True, False)
            body0(NG - 1, False, True, False)
            body0(NG, False, True, False)
            body0(NG + 1, False, True, False)
            with sp.Fori(NG + 2, 2 * NG - 1) as i:
                store(i - 2 - NG)
                body1(i)
            for g in (NG - 3, NG - 2, NG - 1):
                store(g)
            sp.wait_ge(s_stored, 16 * NG)
            settled(sp, 16 * NG)

        @block.tensor
        def _(pe):
            mm, transpose = nc.tensor.matmul, nc.tensor.transpose

            pe.wait_ge(s_ident, 2)
            pe.wait_ge(s_vec_rows, 16 * 9)
            transpose(N_ps[:, 0:NVEC], vec_rows[:, :], ident[0:NVEC, 0:NVEC])
            pe.wait_ge(s_rows_p, 1)
            transpose(N_ps[:, 32:32 + NVEC], vec_rows_p[:, :], ident[0:NVEC, 0:NVEC]).then_inc(s_vec_T, 1)
            pe.wait_ge(s_weights, 16 * 9)
            for c, bank in enumerate(wbanks):
                for n in range(4 * c, min(4 * c + 4, NW)):
                    last = transpose(bank[:, (n % 4) * 128:(n % 4 + 1) * 128], wraw[:, n * 128:(n + 1) * 128], ident[:])
                last.then_inc(s_w_T, 1)
            pe.wait_ge(s_w_sb, len(wbanks))
            pe.wait_ge(s_vecs, 1)

            def transpose_group(dst, src):
                for b in range(GB):
                    last = transpose(dst[:, b * 128:(b + 1) * 128], src[:, b * 128:(b + 1) * 128], ident[:])
                return last

            def scores(i, u):
                b, c = divmod(u, UB)
                if c == 0:
                    pe.wait_ge(s_stack[b], 32 * (i + 1))
                if above_zero(NU * i + u - 1):
                    pe.wait_ge(s_masked, NU * i + u - 1)
                for j in range(UH):
                    h = c * UH + j
                    last = mm(S_ps[u % 2][:, j * S:(j + 1) * S], q_st[:, b, h], k_st[:, b, h], start=True, stop=True)
                last.then_inc(s_scores, 1)

            def turn(i, u):
                pe.wait_ge(s_shifted, NU * i + u + 1)
                if above_zero(NU * i + u - 1):
                    pe.wait_ge(s_exps, NU * i + u - 1)
                for j in range(UH):
                    last = transpose(E_ps[u % 2][:, j * S:(j + 1) * S], t_sb[:, u % RT, j], ident[:])
                last.then_inc(s_turned, 1)

            def values(i, u):
                b, c = divmod(u, UB)
                pe.wait_ge(s_exps, NU * i + u + 1)
                if c == 0:
                    pe.wait_ge(s_v_aug, GB * i + b + 1)
                    if above_zero(GB * i + b):
                        pe.wait_ge(s_o_out, GB * i + b)
                for j in range(UH):
                    last = mm(O_ps[32 * j:32 * j + VW, c * S:(c + 1) * S], v_aug[:, b, c * UH + j],
                              p_sb[:, u % RP, j * S:(j + 1) * S], start=True, stop=True)
                last.then_inc(s_values, 1)

            def o_turn(i, b):
                pe.wait_ge(s_o_out, GB * i + b + 1)
                if above_zero(GB * i + b):
                    pe.wait_ge(s_aT, GB * i + b)
                for c in range(UB):
                    last = transpose(N_ps[:, c * 128:(c + 1) * 128], oT_aug[:, c * 128:(c + 1) * 128], ident[:])
                last.then_inc(s_o_turned, 1)

            def o_back(i, b):
                pe.wait_ge(s_o_n, GB * i + b + 1)
                transpose(N_ps[:, 0:128], o_n[:, :, :].rearrange("p h d -> p (h d)"), ident[:]).then_inc(s_o_back, 1)

            def side(i, u, L, Lp, pre, l2):
                if u == 0 and l2:
                    if pre:
                        pe.wait_ge(s_xg, i + 1)
                    else:
                        pe.wait_ge(s_xg, NG)
                    if not pre:
                        pe.wait_ge(s_R5_out, i - 2)
                    pe.wait_ge(s_xn2, i - 1)
                    transpose_group(BANK["R2"], flat(xn2)).then_inc(s_R2_ready, 1)
                if u == 1 and l2:
                    pe.wait_ge(s_R2_out, i - 1)
                    for k, (job, ready) in enumerate((("R3a", s_R3a_ready), ("R3b", s_R3b_ready))):
                        if k:
                            pe.wait_ge(s_OP_out, i - 1)
                            if above_zero(2 * i - 4):
                                pe.wait_ge(s_first["q1"], 2 * i - 4)
                        for jj in range(2):
                            last = mm(BANK[job][:, jj * TG:(jj + 1) * TG], W(W_1 + 2 * k + jj), t2T[:], start=True, stop=True)
                        last.then_inc(ready, 1)
                if u == 2 and pre:
                    if l2:
                        pe.wait_ge(s_R3b_out, 2 * i - 2)
                    else:
                        if above_zero(2 * i + 2):
                            pe.wait_ge(s_first["k1"], 2 * i + 2)
                        if above_zero(i - 1):
                            pe.wait_ge(s_OP_out, i - 1)
                    pe.wait_ge(s_xn, i + 2)
                    transpose_group(BANK["P1"], flat(xn))
                    pe.wait_ge(s_c_in, 16 * (i + 2))
                    transpose_group(BANK["P1"][:, TG:2 * TG], flat(c_in)).then_inc(s_P1_ready, 1)
                if u == 3 and pre:
                    if l2:
                        if above_zero(2 * i - 2):
                            pe.wait_ge(s_R3a_out, 2 * i - 2)
                    else:
                        if above_zero(i + 1):
                            pe.wait_ge(s_xg, i + 1)
                    pe.wait_ge(s_P1_out, 2 * (i + 2))
                    mm(BANK["QK"][:, 0:TG], W(W_K), tT[:], start=True, stop=True)
                    mm(BANK["QK"][:, TG:2 * TG], W(W_Q), tT[:], start=True, stop=True).then_inc(s_QK_ready, 1)
                if u == 4 and l2:
                    if pre:
                        pe.wait_ge(s_P1_out, 2 * i + 4)
                    else:
                        pe.wait_ge(s_R3b_out, 2 * i - 2)
                    pe.wait_ge(s_R3a_out, 2 * (i - 1))
                    pe.wait_ge(s_R3b_out, 2 * (i - 1))
                    for b in range(GB):
                        for j in range(NJ):
                            last = mm(BANK["R4"][:, b * D:(b + 1) * D], hT[:, j, b * S:(b + 1) * S], W(W_2 + j),
                                      start=(j == 0), stop=(j == NJ - 1))
                    last.then_inc(s_R4_ready, 1)
                if u == 5 and pre:
                    pe.wait_ge(s_first["k0"], 2 * i + 4)
                    pe.wait_ge(s_first["q0"], 2 * i + 4)
                    for k, (t, w) in enumerate(((tT, W_V), (cT, W_V1))):
                        for b in range(GB):
                            at = (k * GB + b) * D
                            last = mm(BANK["V"][:, at:at + D], t[:, b * S:(b + 1) * S], W(w), start=True, stop=True)
                    last.then_inc(s_V_ready, 1)
                if u == 5 and pre:
                    if l2:
                        pe.wait_ge(s_x3, i - 1)
                    else:
                        pe.wait_ge(s_P1_out, 2 * i + 4)
                    mm(BANK["K1"][:, 0:TG], W(W_K1), cT[:], start=True, stop=True).then_inc(s_k1_ready, 1)
                if u == 6 and l2:
                    if pre:
                        pe.wait_ge(s_V_out, 2 * i + 4)
                    else:
                        pe.wait_ge(s_R3a_out, 2 * i - 2)
                    pe.wait_ge(s_x3, i - 1)
                    transpose_group(BANK["R5"], x3).then_inc(s_R5_ready, 1)
                if u == 6 and Lp is not None:
                    if pre:
                        pe.wait_ge(s_first["k1"], 2 * i + 4)
                    elif l2:
                        pe.wait_ge(s_x3, i - 1)
                    else:
                        pe.wait_ge(s_OP_out, i - 1)
                        pe.wait_ge(s_first["q1"], 2 * NG)
                    pe.wait_ge(s_aT, GB * i)
                    for b in range(GB):
                        last = mm(BANK["OP"][:, b * D:(b + 1) * D], aT[:, b], W(W_O1 if Lp else W_O), start=True, stop=True)
                    last.then_inc(s_OP_ready, 1)
                if u == 7 and pre:
                    if l2:
                        pe.wait_ge(s_R5_out, i - 1)
                    else:
                        pe.wait_ge(s_V_out, 2 * i + 4)
                    for b in range(GB):
                        last = mm(BANK["G"][:, b * D:(b + 1) * D], cT[:, b * S:(b + 1) * S], W(W_G), start=True, stop=True)
                    last.then_inc(s_G_ready, 1)
                if u == 7 and l2:
                    pe.wait_ge(s_OP_out, i)
                    pe.wait_ge(s_R5_out, i - 1)
                    mm(BANK["Q1"][:, 0:TG], W(W_Q1), x3T[:], start=True, stop=True).then_inc(s_q1_ready, 1)

            def body(i, L, Lp, pre, l2):
                for u in range(NU):
                    if L is not None:
                        scores(i, u)
                    if u >= LT and L is not None:
                        turn(i, u - LT)
                    elif u < LT and Lp is not None:
                        turn(i - 1, u - LT + NU)
                    if u >= LP and L is not None:
                        values(i, u - LP)
                    elif u < LP and Lp is not None:
                        values(i - 1, u - LP + NU)
                    if Lp is not None and u in (0, 4):
                        o_turn(i - 1, u // 4)
                    side(i, u, L, Lp, pre, l2)
                    if Lp is not None and u in (0, 4):
                        o_back(i - 1, u // 4)

            schedule(pe, body)

        @block.scalar
        def _(act):
            A = nc.scalar.activation
            for r, v, k in ((BQ, bq, 1), (BK, bk, 1), (BV, bv, 1), (G1, g1, 1), (BE1, be1, 1), (G2, g2, 1),
                            (BE2, be2, 1), (B1, b1, NJ), (BQ1, bqkv1, 3)):
                act.dma_start(vec_rows[r:r + k], row(v)).then_inc(s_vec_rows, 16)
            for r, v in enumerate((bo, bg, b2, bo1, gam, bet)):
                act.dma_start(rep[:, r], row(v).to_broadcast([128, 128])).then_inc(s_rep, 16)

            act.wait_ge(s_w_T, 1)
            for n in (W_Q, W_K):
                A(W(n).rearrange("p (d h) -> p d h", d=HD),
                  wbanks[0][:, n * 128:(n + 1) * 128].rearrange("p (h d) -> p d h", d=HD), ACT.Copy)
            A(W(2, 2), wbanks[0][:, 256:512], ACT.Copy).then_inc(s_w_sb, 1)
            for c in (1, 2):
                act.wait_ge(s_w_T, c + 1)
                A(W(4 * c, 4), wbanks[c][:, :], ACT.Copy).then_inc(s_w_sb, 1)
            act.wait_ge(s_vecs, 2)
            act.wait_ge(s_ones, 1)

            def exps(i, u):
                act.wait_ge(s_turned, NU * i + u + 1)
                if above_zero(NU * i + u + 1 - RP):
                    act.wait_ge(s_values, NU * i + u + 1 - RP)
                A(p_sb[:, u % RP], E_ps[u % 2][:, :], ACT.Exp).then_inc(s_exps, 1)

            def o_out(i, b):
                act.wait_ge(s_values, NU * i + UB * (b + 1))
                A(oT_aug[:], O_ps[:, :], ACT.Copy).then_inc(s_o_out, 1)

            def a_out(i, b, L):
                act.wait_ge(s_o_back, GB * i + b + 1)
                bias = vec[:, BV1:BV1 + 1] if L else vec[:, BV:BV + 1]
                A(aT[:, b], N_ps[:, 0:128], ACT.Identity, bias=bias).then_inc(s_aT, 1)

            def v_copy(i, b, L):
                if above_zero(NU * (i - 1) + UB * (b + 1)):
                    act.wait_ge(s_values, NU * (i - 1) + UB * (b + 1))
                act.wait_ge(s_V_out, 2 * NG if L else 2 * (i + 1))
                src = v_all[:, bass.ts(GB * i + b, D)].rearrange("p (h d) -> p h d", d=HD)
                A(v_aug[:, b, :, 0:HD], src, ACT.Copy).then_inc(s_v_aug, 1)

            def split_first(kind, grp, ready, src, bias, scale):
                act.wait_ge(ready, grp + 1)
                if above_zero(WROTE * grp):
                    act.wait_ge(s_wrote[kind], WROTE * grp)
                A(parts[kind][:, 0], src, ACT.Identity, bias=bias, scale=scale).then_inc(s_first[kind], 1)
                A(full[kind][:], src, ACT.Identity, bias=bias, scale=scale).then_inc(s_first[kind], 1)

            def split_second(kind, grp):
                act.wait_ge(s_resid[kind], grp + 1)
                A(parts[kind][:, 1], resid[kind][:], ACT.Copy).then_inc(s_part2[kind], 1)

            col = lambda t, n: t[:, n:n + 1]

            def side(i, u, L, Lp, pre, l2):
                if u == 0 and l2:
                    act.wait_ge(s_R2_ready, i - 1)
                    A(t2T[:], BANK["R2"][:, 0:TG], ACT.Identity, bias=col(vec, BE2), scale=col(vec, G2)).then_inc(s_R2_out, 1)
                if u == 1 and l2:
                    act.wait_ge(s_R3a_ready, i - 1)
                    for j in range(2):
                        A(hT[:, j], BANK["R3a"][:, j * TG:(j + 1) * TG], ACT.Relu, bias=col(vec, B1 + j)).then_inc(s_R3a_out, 1)
                if u == 2 and pre:
                    act.wait_ge(s_P1_ready, i + 2)
                    A(tT[:], BANK["P1"][:, 0:TG], ACT.Identity, bias=col(vec, BE1), scale=col(vec, G1)).then_inc(s_P1_out, 1)
                    A(cT[:], BANK["P1"][:, TG:2 * TG], ACT.Copy).then_inc(s_P1_out, 1)
                if u == 3 and pre:
                    split_first("k0", i + 1, s_QK_ready, BANK["QK"][:, 0:TG], col(vec_p, BK), 1.0)
                    split_first("q0", i + 1, s_QK_ready, BANK["QK"][:, TG:2 * TG], col(vec_ps, BQ), SCALE)
                if u == 4 and pre:
                    split_second("k0", i + 1)
                    split_second("q0", i + 1)
                if u == 5 and pre:
                    act.wait_ge(s_V_ready, i + 2)
                    for k in range(2):
                        A(v_all[:, bass.ts(i + 1 + NG * k, TG)], BANK["V"][:, k * TG:(k + 1) * TG], ACT.Copy).then_inc(s_V_out, 1)
                if u == 5 and pre:
                    split_first("k1", i + 1, s_k1_ready, BANK["K1"][:, 0:TG], col(vec_p, BK1), 1.0)
                if u == 6 and l2:
                    act.wait_ge(s_R5_ready, i - 1)
                    A(x3T[:], BANK["R5"][:, 0:TG], ACT.Copy).then_inc(s_R5_out, 1)
                if u == 6 and pre:
                    split_second("k1", i + 1)
                if u == 7 and l2:
                    split_first("q1", i - 2, s_q1_ready, BANK["Q1"][:, 0:TG], col(vec_ps, BQ1), SCALE)
                    split_second("q1", i - 2)

            def body(i, L, Lp, pre, l2):
                for u in range(NU):
                    if u >= LT and L is not None:
                        exps(i, u - LT)
                    elif u < LT and Lp is not None:
                        exps(i - 1, u - LT + NU)
                    if Lp is not None and u == 3:
                        o_out(i - 1, 1)
                    if L is not None and u == 7:
                        o_out(i, 0)
                    side(i, u, L, Lp, pre, l2)
                    if L is not None and u in (1, 5):
                        v_copy(i, u // 4, L)
                    if Lp is not None and u in (0, 4):
                        a_out(i - 1, u // 4, Lp)

            schedule(act, body)

        @block.vector
        def _(dve):
            V = nc.vector
            V.memset(q_st[:, :, :, :], 0.0).then_inc(s_zeroed, 1)
            dve.wait_ge(s_vec_rows, 16 * 9)
            V.tensor_copy(vec_rows_p[:, :].rearrange("r (d h) -> r d h", d=HD),
                          vec_rows[:, :].rearrange("r (h d) -> r d h", d=HD)).then_inc(s_rows_p, 1)
            dve.wait_ge(s_vec_T, 1)
            V.tensor_copy(vec[:], N_ps[:, 0:NVEC])
            V.tensor_copy(vec_p[:], N_ps[:, 32:32 + NVEC]).then_inc(s_vecs, 1)
            dve.wait_ge(s_vecs, 1)
            V.tensor_scalar(vec_ps[:], vec_p[:], SCALE, None, ALU.mult).then_inc(s_vecs, 1)
            dve.wait_ge(s_w_T, 4)
            V.tensor_copy(W(12), wbanks[3][:, 0:128])
            for n in (W_Q1, W_K1):
                V.tensor_copy(W(n).rearrange("p (d h) -> p d h", d=HD),
                              wbanks[3][:, (n - 12) * 128:(n - 11) * 128].rearrange("p (h d) -> p d h", d=HD))
            V.tensor_copy(W(15), wbanks[3][:, 384:512]).then_inc(s_w_sb, 1)
            dve.wait_ge(s_w_T, 5)
            V.tensor_copy(W(16), wbanks[4][:, 0:128]).then_inc(s_w_sb, 1)
            dve.wait_ge(s_vecs, 2)

            def mask_bias(grp, b):
                dve.wait_ge(s_m_in[b], 16 * (grp + 1))
                V.tensor_scalar(mbias[:, b], m_in[:, b], -1.0, BIG, ALU.add, ALU.mult).then_inc(s_mbias[b], 1)

            def masked_max(i, u, L):
                b = u // UB
                dve.wait_ge(s_scores, NU * i + u + 1)
                if above_zero(NU * i + u + 1 - RT):
                    dve.wait_ge(s_turned, NU * i + u + 1 - RT)
                if L == 0 and u % UB == 0:
                    dve.wait_ge(s_mbias[b], i + 1)
                settled(dve, i)
                for j in range(UH):
                    t, s, m = t_sb[:, u % RT, j], S_ps[u % 2][:, j * S:(j + 1) * S], mx[:, u % RT, j:j + 1]
                    if L == 0:
                        last = V.tensor_tensor_reduce(t, s, mbias[:, b], 1.0, -3.4e38, ALU.add, ALU.max, m)
                    else:
                        last = V.tensor_scalar(t, s, 1.0, None, ALU.mult, ALU.max, accum_out=m)
                last.then_inc(s_masked, 1)

            def normalise(i, b):
                dve.wait_ge(s_o_turned, GB * i + b + 1)
                nv = N_ps[:, :].rearrange("p (h w) -> p h w", w=VW)
                V.reciprocal(rden[:], nv[:, :, HD]).then_inc(s_rden, 1)
                dve.wait_ge(s_rden, GB * i + b + 1)
                V.tensor_tensor(o_n[:, :, :], nv[:, :, 0:HD], rden[:].unsqueeze(2).to_broadcast([128, NH, HD]),
                                ALU.mult).then_inc(s_o_n, 1)

            def norm_stats(k, src, n):
                for b in range(GB):
                    last = V.bn_stats(stats[k][:, b], src[:, b * D:(b + 1) * D])
                last.then_inc(s_ln[k], 1)
                dve.wait_ge(s_ln[k], 2 * n + 1)
                settled(dve, n)
                for b in range(GB):
                    last = V.bn_aggr(mv[k][:, b], stats[k][:, b])
                last.then_inc(s_ln[k], 1)

            def norm_apply(k, dst, src, n, done):
                dve.wait_ge(s_rstd[k], n + 1)
                for b in range(GB):
                    last = V.tensor_scalar(dst[:, b], src[:, b * D:(b + 1) * D], mv[k][:, b, 0:1], rstd[k][:, b:b + 1],
                                           ALU.subtract, ALU.mult)
                last.then_inc(done, 1)

            def split_resid(kind, grp):
                dve.wait_ge(s_first[kind], 2 * (grp + 1))
                V.tensor_tensor(resid[kind][:], full[kind][:], parts[kind][:, 0], ALU.subtract).then_inc(s_resid[kind], 1)

            def split_third(kind, grp):
                dve.wait_ge(s_part2[kind], grp + 1)
                V.tensor_tensor(parts[kind][:, 2], resid[kind][:], parts[kind][:, 1], ALU.subtract).then_inc(s_part3[kind], 1)

            def side(i, u, L, Lp, pre, l2):
                if L == 0 and u == 1:
                    mask_bias(i, 1)
                if pre and u == 5:
                    mask_bias(i + 1, 0)
                if u == 0 and pre:
                    dve.wait_ge(s_x_in, 16 * (i + 2))
                    norm_stats("a", flat(x_in), i + 1)
                if u == 1 and pre:
                    if above_zero(i + 1):
                        dve.wait_ge(s_P1_ready, i + 1)
                    norm_apply("a", xn, flat(x_in), i + 1, s_xn)
                if u == 1 and l2:
                    dve.wait_ge(s_R3b_ready, i - 1)
                    for j in range(2):
                        V.tensor_scalar(hT[:, 2 + j], BANK["R3b"][:, j * TG:(j + 1) * TG], vec[:, B1 + 2 + j:B1 + 3 + j], 0.0,
                                        ALU.add, ALU.max).then_inc(s_R3b_out, 1)
                if u == 3 and pre:
                    split_resid("k0", i + 1)
                    split_resid("q0", i + 1)
                if u == 4 and pre:
                    split_third("k0", i + 1)
                    split_third("q0", i + 1)
                if u == 4 and l2:
                    dve.wait_ge(s_R4_ready, i - 1)
                    dve.wait_ge(s_x2b, i - 1)
                    if above_zero(i - 2):
                        dve.wait_ge(s_x3b, i - 2)
                    V.tensor_tensor(x3[:], BANK["R4"][:, 0:TG], x2b[:], ALU.add).then_inc(s_x3, 1)
                if u == 5 and pre:
                    split_resid("k1", i + 1)
                if u == 6 and pre:
                    split_third("k1", i + 1)
                if u == 6 and Lp is not None:
                    dve.wait_ge(s_OP_ready, i)
                    if Lp == 0:
                        if above_zero(i - 1):
                            dve.wait_ge(s_x2b, i - 1)
                        dve.wait_ge(s_xg, i)
                        res = xg_all[:, bass.ts(i - 1, TG)]
                    else:
                        dve.wait_ge(s_x2b, NG)
                        dve.wait_ge(s_x3b, NG)
                        res = x3b_all[:, bass.ts(i - 1 - NG, TG)]
                    V.tensor_tensor(x2[:], BANK["OP"][:, 0:TG], res, ALU.add).then_inc(s_OP_out, 1)
                    dve.wait_ge(s_OP_out, i)
                    norm_stats("b", x2, i - 1)
                if u == 7 and pre:
                    dve.wait_ge(s_G_ready, i + 2)
                    dve.wait_ge(s_xb, i + 2)
                    V.tensor_tensor(xg_all[:, bass.ts(i + 1, TG)], BANK["G"][:, 0:TG], xb[:], ALU.add).then_inc(s_xg, 1)
                if u == 7 and Lp is not None:
                    if Lp == 0:
                        if above_zero(i - 1):
                            dve.wait_ge(s_R2_ready, i - 1)
                    else:
                        dve.wait_ge(s_R2_ready, NG)
                        if above_zero(i - 1 - NG):
                            dve.wait_ge(s_yg, i - 1 - NG)
                    norm_apply("b", xn2, x2, i - 1, s_xn2)
                if u == 7 and l2:
                    split_resid("q1", i - 2)
                    split_third("q1", i - 2)

            def body(i, L, Lp, pre, l2):
                for u in range(NU):
                    if L is not None:
                        masked_max(i, u, L)
                    if Lp is not None and u in (0, 4):
                        normalise(i - 1, u // 4)
                    side(i, u, L, Lp, pre, l2)

            schedule(dve, body)

        @block.gpsimd
        def _(pool):
            G = nc.gpsimd
            G.memset(ident[:], 0.0).then_inc(s_ident, 1)
            pool.wait_ge(s_ident, 1)
            G.affine_select(out=ident[:], in_=ident[:], compare_op=ALU.not_equal, fill=1.0, base=0, pattern=[[-1, 128]],
                            channel_multiplier=1).then_inc(s_ident, 1)
            G.memset(expo[:], -0.5)
            G.memset(k_st[:, :, :, :], 0.0).then_inc(s_zeroed, 1)
            G.memset(v_aug[:, :, :, :], 1.0).then_inc(s_ones, 1)
            pool.wait_ge(s_rep, 16 * NREP)
            G.tensor_tensor(bias_og[:], rep[:, R_BO], rep[:, R_BG], ALU.add).then_inc(s_bias_og, 1)
            pool.wait_ge(s_bias_og, 1)
            pool.wait_ge(s_ones, 1)
            per_row = lambda t: t.unsqueeze(1).to_broadcast([128, GB, D])
            grouped = lambda t: t.rearrange("p (b d) -> p b d", b=GB)

            def shift(i, u):
                pool.wait_ge(s_masked, NU * i + u + 1)
                t = t_sb[:, u % RT]
                G.tensor_tensor(t, t, mx[:, u % RT].unsqueeze(2).to_broadcast([128, UH, S]), ALU.subtract).then_inc(s_shifted, 1)

            def inverse_root(k, n):
                pool.wait_ge(s_ln[k], 2 * n + 2)
                settled(pool, n)
                G.tensor_scalar(ve[k][:], mv[k][:, :, 1], EPS, None, ALU.add).then_inc(s_ve[k], 1)
                pool.wait_ge(s_ve[k], n + 1)
                G.tensor_tensor(rstd[k][:], ve[k][:], expo[:], ALU.pow).then_inc(s_rstd[k], 1)

            def body(i, L, Lp, pre, l2):
                for u in range(NU):
                    if u == 0 and pre:
                        inverse_root("a", i + 1)
                    if L is not None:
                        shift(i, u)
                    if u == 1 and pre:
                        pool.wait_ge(s_x_in, 16 * (i + 2))
                        if above_zero(i + 1):
                            pool.wait_ge(s_xg, i + 1)
                        G.tensor_tensor(grouped(xb[:]), x_in[:, :, :], per_row(bias_og[:]), ALU.add).then_inc(s_xb, 1)
                    if u == 5 and l2:
                        pool.wait_ge(s_x3, i - 1)
                        G.tensor_tensor(grouped(x3b_all[:, bass.ts(i - 2, TG)]), grouped(x3[:]), per_row(rep[:, R_BO1]),
                                        ALU.add).then_inc(s_x3b, 1)
                    if u == 6 and Lp is not None:
                        inverse_root("b", i - 1)
                    if u == 7 and Lp == 0:
                        pool.wait_ge(s_OP_out, i)
                        if above_zero(i - 1):
                            pool.wait_ge(s_x3, i - 1)
                        G.tensor_tensor(grouped(x2b[:]), grouped(x2[:]), per_row(rep[:, R_B2]), ALU.add).then_inc(s_x2b, 1)
                    if u == 7 and Lp == 1:
                        pool.wait_ge(s_xn2, i)
                        G.tensor_tensor(yg[:, :, :], xn2[:, :, :], per_row(rep[:, R_GAM]), ALU.mult).then_inc(s_yg, 1)
                        pool.wait_ge(s_yg, i - NG)
                        if above_zero(16 * (i - 1 - NG)):
                            pool.wait_ge(s_stored, 16 * (i - 1 - NG))
                        G.tensor_tensor(y_out[:, :, :], yg[:, :, :], per_row(rep[:, R_BET]), ALU.add).then_inc(s_y_out, 1)

            schedule(pool, body)


_INS = ["x", "ctx_1024", "mask_BxSxS2_fk0", "L0_xattn_Wq", "L0_xattn_bq", "L0_xattn_Wk", "L0_xattn_bk", "L0_xattn_Wv",
        "L0_xattn_bv", "L0_xattn_Wo", "L0_xattn_bo", "L0_xattn_Wg", "L0_xattn_bg", "L0_xattn_W1", "L0_xattn_b1",
        "L0_xattn_W2", "L0_xattn_b2", "L0_xattn_g1", "L0_xattn_be1", "L0_xattn_g2", "L0_xattn_be2", "L1_xattn_W_qkv",
        "L1_xattn_b_qkv", "L1_xattn_W_o", "L1_xattn_b_o", "L1_xattn_ln_gamma", "L1_xattn_ln_beta"]
_OUTS = [((NB, S, D), "float32")]


def kernel(**inputs):
    import numpy as _np
    import concourse.bacc as _bacc
    from concourse import mybir as _mybir
    from concourse.bass_utils import run_bass_kernel_spmd as _run

    nc = _bacc.Bacc("TRN2", target_bir_lowering=False, num_devices=1)
    arrays, args = {}, []
    for name in _INS:
        a = _np.ascontiguousarray(inputs[name])
        arrays[f"in_{name}_dram"] = a
        args.append(nc.dram_tensor(f"in_{name}_dram", a.shape, _mybir.dt.from_np(a.dtype), kind="ExternalInput").ap())
    for n, (shape, dtype) in enumerate(_OUTS):
        dt = _mybir.dt.from_np(_np.dtype(dtype))
        args.append(nc.dram_tensor(f"out_{n}_dram", shape, dt, kind="ExternalOutput").ap())
    build(nc, *args)
    r = _run(nc, [arrays], core_ids=[0])
    return tuple(r.results[0][f"out_{n}_dram"] for n in range(len(_OUTS)))[0]
```

```python
import concourse.bass as bass
from concourse import mybir
from contextlib import ExitStack

F32 = mybir.dt.float32
BF16 = mybir.dt.bfloat16
ALU = mybir.AluOpType
ACT = mybir.ActivationFunctionType

NB, S, D = 16, 128, 128
NH, HD, FF = 16, 8, 512
GB = 2
NG = NB // GB
TG = GB * S
UH = 4
UB = NH // UH
NU = GB * UB
NJ = FF // 128
NP = 3
NSLOT = 6
Q_PART, K_PART = (0, 1, 2, 0, 1, 0), (0, 0, 0, 1, 1, 2)
VW = 32
SCALE = HD ** -0.5
EPS = 1e-5
BIG = 1.0e9
LT, LP = 2, 4
RT, RP = 4, 4
STACKED = 16 * NSLOT

BQ, BK, BV, G1, BE1, G2, BE2, B1, BQ1, BK1, BV1 = 0, 1, 2, 3, 4, 5, 6, 7, 11, 12, 13
NVEC = 14
R_BO, R_BG, R_B2, R_BO1, R_GAM, R_BET, NREP = 0, 1, 2, 3, 4, 5, 6
W_Q, W_K, W_V, W_O, W_G, W_1, W_2, W_Q1, W_K1, W_V1, W_O1, NW = 0, 1, 2, 3, 4, 5, 9, 13, 14, 15, 16, 17


def build(nc, x, ctx_, mask, Wq, bq, Wk, bk, Wv, bv, Wo, bo, Wg, bg, W1, b1, W2, b2, g1, be1, g2, be2,
          Wqkv1, bqkv1, Wo1, bo1, gam, bet, out):
    x_v = x.rearrange("(g b) s d -> g s b d", b=GB)
    c_v = ctx_.rearrange("(g b) s d -> g s b d", b=GB)
    o_v = out.rearrange("(g b) s d -> g s b d", b=GB)
    row = lambda a: a.rearrange("(r n) -> r n", n=128)

    with ExitStack() as es:
        sb = lambda name, shape, dt=F32: es.enter_context(nc.sbuf_tensor(name, shape, dt))
        ps = lambda name: es.enter_context(nc.psum_tensor(name, [128, 512], F32))

        def above_zero(count):
            return not isinstance(count, int) or count > 0

        def settled(eng, i):
            if not isinstance(i, int):
                eng.sem_inc(s_settled[eng.engine.name], 1)

        sem = lambda name: es.enter_context(nc.semaphore(name))
        s_weights, s_vec_rows, s_rep = sem("weights_loaded"), sem("vec_rows_loaded"), sem("rep_loaded")
        s_ident, s_zeroed, s_ones = sem("ident_made"), sem("stacks_zeroed"), sem("ones_set")
        s_rows_p, s_vec_T, s_vecs = sem("rows_permuted"), sem("vectors_turned"), sem("vectors_in_sbuf")
        s_w_T, s_w_sb, s_bias_og = sem("weights_turned"), sem("weights_in_sbuf"), sem("bias_og_made")
        s_x_in, s_c_in, s_stored = sem("x_loaded"), sem("context_loaded"), sem("y_stored")
        s_m_in = [sem(f"mask_loaded{b}") for b in range(GB)]
        s_scores, s_masked, s_shifted = sem("scores_ready"), sem("masked_and_max"), sem("max_subtracted")
        s_turned, s_exps, s_values = sem("scores_turned"), sem("exps_ready"), sem("values_summed")
        s_o_out, s_o_turned, s_rden = sem("o_in_sbuf"), sem("o_turned"), sem("sums_inverted")
        s_o_n, s_o_back, s_aT, s_v_aug = sem("o_normalised"), sem("o_turned_back"), sem("aT_in_sbuf"), sem("v_in_place")
        s_mbias = [sem(f"mask_bias{b}") for b in range(GB)]
        by_kind = lambda name: {k: sem(f"{name}_{k}") for k in "kq"}
        s_first, s_resid, s_part2 = by_kind("split1"), by_kind("resid"), by_kind("split2")
        s_part3, s_stack = by_kind("split3"), by_kind("stacked")
        by_norm = lambda name: {k: sem(f"{name}_{k}") for k in "ab"}
        s_ln, s_ve, s_rstd = by_norm("norm_stats"), by_norm("norm_var"), by_norm("norm_rstd")
        s_P1_ready, s_P1_out = sem("P1_ready"), sem("P1_out")
        s_QK_ready, s_V_ready = sem("QK_ready"), sem("V_ready")
        s_c_kept, s_c_back = sem("context_kept"), sem("context_back")
        s_R2_ready, s_R2_out = sem("R2_ready"), sem("R2_out")
        s_R3a_ready, s_R3a_out = sem("R3a_ready"), sem("R3a_out")
        s_R3b_ready, s_R3b_out = sem("R3b_ready"), sem("R3b_out")
        s_R4_ready, s_R5_ready, s_R5_out = sem("R4_ready"), sem("R5_ready"), sem("R5_out")
        s_OP_ready, s_OP_out = sem("OP_ready"), sem("OP_out")
        s_xn, s_xb, s_xg, s_xn2 = sem("xn_made"), sem("xb_made"), sem("xg_made"), sem("xn2_made")
        s_x2b, s_x3, s_x3b, s_yg, s_y_out = sem("x2b_made"), sem("x3_made"), sem("x3b_made"), sem("yg_made"), sem("y_made")
        s_settled = {e: sem(f"settled_{e}") for e in ("SP", "DVE", "Pool")}

        ident = sb("ident", [128, 128])
        wraw = sb("wraw", [128, NW * 128])
        wT = sb("wT", [128, NW * 128])
        vec_rows = sb("vec_rows", [NVEC, 128])
        vec_rows_p = sb("vec_rows_p", [NVEC, 128])
        vec = sb("vec", [128, NVEC])
        vec_p = sb("vec_p", [128, NVEC])
        vec_ps = sb("vec_ps", [128, NVEC])
        rep = sb("rep", [128, NREP, 128])
        bias_og = sb("bias_og", [128, 128])
        expo = sb("expo", [128, GB])
        W = lambda n, k=1: wT[:, n * 128:(n + k) * 128]
        x_in = sb("x_in", [128, GB, D])
        c_in = sb("c_in", [128, GB, D])
        m_in = sb("m_in", [128, GB, S])
        mbias = sb("mbias", [128, GB, S])
        xg_all = sb("xg_all", [128, NG * TG])
        x3b_all = sb("x3b_all", [128, NG * TG])
        xn = sb("xn", [128, GB, D])
        xb = sb("xb", [128, TG])
        tT = sb("tT", [128, TG])
        cT = sb("cT", [128, TG])
        cT_all = sb("cT_all", [128, NG * TG])
        x3T_all = sb("x3T_all", [128, NG * TG])
        full = {k: sb(f"full_{k}", [128, TG]) for k in "kq"}
        resid = {k: sb(f"resid_{k}", [128, TG]) for k in "kq"}
        parts = {k: sb(f"parts_{k}", [128, NP, TG], BF16) for k in "kq"}
        q_st = sb("q_st", [128, 2, NH, TG], BF16)
        k_st = sb("k_st", [128, 2, NH, TG], BF16)
        v_aug = sb("v_aug", [128, 2, GB, NH, VW])
        t_sb = sb("t_sb", [128, RT, UH, S])
        mx = sb("mx", [128, RT, UH])
        p_sb = sb("p_sb", [128, RP, UH * S])
        oT_aug = sb("oT_aug", [128, 512])
        rden = sb("rden", [128, NH])
        o_n = sb("o_n", [128, NH, HD])
        aT = sb("aT", [128, GB, S])
        stats = {k: sb(f"stats_{k}", [128, GB, 6]) for k in "ab"}
        mv = {k: sb(f"mv_{k}", [128, GB, 2]) for k in "ab"}
        ve = {k: sb(f"ve_{k}", [128, GB]) for k in "ab"}
        rstd = {k: sb(f"rstd_{k}", [128, GB]) for k in "ab"}
        x2 = sb("x2", [128, TG])
        x2b = sb("x2b", [128, TG])
        xn2 = sb("xn2", [128, GB, D])
        t2T = sb("t2T", [128, TG])
        hT = sb("hT", [128, NJ, TG])
        x3 = sb("x3", [128, TG])
        yg = sb("yg", [128, GB, D])
        y_out = sb("y_out", [128, GB, D])

        S_ps = [ps("S0"), ps("S1")]
        E_ps = [ps("E0"), ps("E1")]
        O_ps = ps("O")
        N_ps = ps("N")
        D_ps = [ps("D0"), ps("D1")]
        BANK = {"R2": 0, "R3a": 0, "R4": 0, "R5": 0, "QK": 0,
                "R3b": 1, "V": 1, "P1": 1, "OP": 1}
        BANK = {job: D_ps[n] for job, n in BANK.items()}
        wbanks = [D_ps[0], D_ps[1], S_ps[0], S_ps[1], O_ps]

        block = es.enter_context(nc.Block())

        def schedule(eng, body):
            body(-2, None, None, 0, None, False)
            body(-1, None, None, 0, 0, False)
            body(0, 0, None, 0, 0, False)
            body(1, 0, 0, 0, 0, False)
            with eng.Fori(1, (NG - 2) // 2) as pair:
                i = 2 * pair
                body(i, 0, 0, 0, 0, True, 0)
                body(i + 1, 0, 0, 0, 0, True, 1)
            body(NG - 2, 0, 0, 1, 0, True)
            body(NG - 1, 0, 0, 1, 1, True)
            body(NG, 1, 0, 1, 1, True)
            body(NG + 1, 1, 1, 1, 1, True)
            with eng.Fori((NG + 2) // 2, (2 * NG - 2) // 2) as pair:
                i = 2 * pair
                body(i, 1, 1, 1, 1, False, 0)
                body(i + 1, 1, 1, 1, 1, False, 1)
            body(2 * NG - 2, 1, 1, None, 1, False)
            body(2 * NG - 1, 1, 1, None, None, False)
            body(2 * NG, None, 1, None, None, False)

        def parity(i, par):
            return i % 2 if par is None else par

        flat = lambda t: t[:, :, :].rearrange("p b d -> p (b d)")
        x3T_of = lambda g: x3T_all[:, bass.ts(g, TG)]

        @block.sync
        def _(sp):
            def stack(i, par):
                if above_zero(NU * (i - 1)):
                    sp.wait_ge(s_scores, NU * (i - 1))
                settled(sp, i)
                for kind, st, part in (("k", k_st, K_PART), ("q", q_st, Q_PART)):
                    sp.wait_ge(s_part3[kind], i + 1)
                    settled(sp, i)
                    for t in range(NSLOT):
                        sp.dma_start(st[HD * t:HD * (t + 1), parity(i, par)], parts[kind][:, part[t]]
                                     ).then_inc(s_stack[kind], 16)

            sp.dma_start(x_in[:], x_v[0]).then_inc(s_x_in, 16)
            sp.dma_start(c_in[:], c_v[0]).then_inc(s_c_in, 16)
            for w, n, k in ((Wq, W_Q, 1), (Wk, W_K, 1), (Wv, W_V, 1), (Wg, W_G, 1), (Wqkv1, W_Q1, 3), (Wo, W_O, 1),
                            (W1, W_1, NJ), (Wo1, W_O1, 1)):
                dst = wraw[:, n * 128:(n + k) * 128].rearrange("p (j n) -> p j n", j=k)
                sp.dma_start(dst, w.rearrange("(j p) n -> p j n", p=128)).then_inc(s_weights, 16)
            sp.dma_start(wraw[:, W_2 * 128:(W_2 + NJ) * 128], W2).then_inc(s_weights, 16)
            sp.dma_start(m_in[:, 0], mask[0]).then_inc(s_m_in[0], 16)
            sp.dma_start(m_in[:, 1], mask[1]).then_inc(s_m_in[1], 16)
            sp.wait_ge(s_zeroed, 4)
            settled(sp, 4)

            def inputs(i):
                sp.wait_ge(s_xb, i)
                settled(sp, i)
                sp.wait_ge(s_xn, i)
                settled(sp, i)
                sp.dma_start(x_in[:], x_v[i]).then_inc(s_x_in, 16)
                sp.wait_ge(s_P1_ready, i)
                settled(sp, i)
                sp.dma_start(c_in[:], c_v[i]).then_inc(s_c_in, 16)

            def mask_load(i, b):
                sp.wait_ge(s_mbias[b], i)
                settled(sp, i)
                sp.dma_start(m_in[:, b], mask[GB * i + b]).then_inc(s_m_in[b], 16)

            def store(g):
                sp.wait_ge(s_y_out, g + 1)
                settled(sp, g + 1)
                sp.dma_start(o_v[g], y_out[:]).then_inc(s_stored, 16)

            def body(i, masks, more, stores, stacks, par=None):
                if stores:
                    store(i - 2 - NG)
                if masks:
                    mask_load(i + 1, 0)
                if stacks:
                    stack(i + 1, None if par is None else 1 - par)
                if masks:
                    mask_load(i + 1, 1)
                if more:
                    inputs(i + 3)

            body(-2, False, True, False, False)
            body(-1, False, True, False, True)
            body(0, True, True, False, True)
            body(1, True, True, False, True)
            with sp.Fori(1, (NG - 4) // 2) as pair:
                i = 2 * pair
                body(i, True, True, False, True, 0)
                body(i + 1, True, True, False, True, 1)
            body(NG - 4, True, True, False, True)
            body(NG - 3, True, False, False, True)
            body(NG - 2, True, False, False, True)
            for i in (NG - 1, NG, NG + 1):
                body(i, False, False, False, True)
            with sp.Fori((NG + 2) // 2, (2 * NG - 2) // 2) as pair:
                i = 2 * pair
                body(i, False, False, True, True, 0)
                body(i + 1, False, False, True, True, 1)
            body(2 * NG - 2, False, False, True, True)
            for g in (NG - 3, NG - 2, NG - 1):
                store(g)
            sp.wait_ge(s_stored, 16 * NG)
            settled(sp, 16 * NG)

        @block.tensor
        def _(pe):
            mm, transpose = nc.tensor.matmul, nc.tensor.transpose

            pe.wait_ge(s_ident, 2)
            pe.wait_ge(s_vec_rows, 16 * 9)
            transpose(N_ps[:, 0:NVEC], vec_rows[:, :], ident[0:NVEC, 0:NVEC])
            pe.wait_ge(s_rows_p, 1)
            transpose(N_ps[:, 32:32 + NVEC], vec_rows_p[:, :], ident[0:NVEC, 0:NVEC]).then_inc(s_vec_T, 1)
            pe.wait_ge(s_weights, 16 * 9)
            for c, bank in enumerate(wbanks):
                for n in range(4 * c, min(4 * c + 4, NW)):
                    last = transpose(bank[:, (n % 4) * 128:(n % 4 + 1) * 128], wraw[:, n * 128:(n + 1) * 128], ident[:])
                last.then_inc(s_w_T, 1)
            pe.wait_ge(s_w_sb, len(wbanks))
            pe.wait_ge(s_vecs, 1)

            def transpose_group(dst, src):
                for b in range(GB):
                    last = transpose(dst[:, b * 128:(b + 1) * 128], src[:, b * 128:(b + 1) * 128], ident[:])
                return last

            def scores(i, u, par):
                b, c = divmod(u, UB)
                if u == 0:
                    pe.wait_ge(s_stack["k"], STACKED * (i + 1))
                    pe.wait_ge(s_stack["q"], STACKED * (i + 1))
                if above_zero(NU * i + u - 1):
                    pe.wait_ge(s_masked, NU * i + u - 1)
                tokens = slice(b * S, (b + 1) * S)
                for j in range(UH):
                    h = c * UH + j
                    last = mm(S_ps[u % 2][:, j * S:(j + 1) * S], q_st[:, par, h, tokens], k_st[:, par, h, tokens],
                              start=True, stop=True)
                last.then_inc(s_scores, 1)

            def turn(i, u):
                pe.wait_ge(s_shifted, NU * i + u + 1)
                if above_zero(NU * i + u - 1):
                    pe.wait_ge(s_exps, NU * i + u - 1)
                for j in range(UH):
                    last = transpose(E_ps[u % 2][:, j * S:(j + 1) * S], t_sb[:, u % RT, j], ident[:])
                last.then_inc(s_turned, 1)

            def values(i, u, par):
                b, c = divmod(u, UB)
                pe.wait_ge(s_exps, NU * i + u + 1)
                if u == 0:
                    pe.wait_ge(s_v_aug, i + 1)
                if c == 0 and above_zero(GB * i + b):
                    pe.wait_ge(s_o_out, GB * i + b)
                for j in range(UH):
                    last = mm(O_ps[32 * j:32 * j + VW, c * S:(c + 1) * S], v_aug[:, par, b, c * UH + j],
                              p_sb[:, u % RP, j * S:(j + 1) * S], start=True, stop=True)
                last.then_inc(s_values, 1)

            def o_turn(i, b):
                pe.wait_ge(s_o_out, GB * i + b + 1)
                if above_zero(GB * i + b):
                    pe.wait_ge(s_aT, GB * i + b)
                for c in range(UB):
                    last = transpose(N_ps[:, c * 128:(c + 1) * 128], oT_aug[:, c * 128:(c + 1) * 128], ident[:])
                last.then_inc(s_o_turned, 1)

            def o_back(i, b):
                pe.wait_ge(s_o_n, GB * i + b + 1)
                transpose(N_ps[:, 0:128], o_n[:, :, :].rearrange("p h d -> p (h d)"), ident[:]).then_inc(s_o_back, 1)

            def side(i, u, L, Lp, A, B, l2):
                if u == 0 and l2:
                    for kind in "kq":
                        pe.wait_ge(s_first[kind], 2 * (i + 2))
                    pe.wait_ge(s_xn2, i - 1)
                    transpose_group(BANK["R2"], flat(xn2)).then_inc(s_R2_ready, 1)
                if u == 1 and l2:
                    pe.wait_ge(s_R2_out, i - 1)
                    for j in range(2):
                        last = mm(BANK["R3a"][:, j * TG:(j + 1) * TG], W(W_1 + j), t2T[:], start=True, stop=True)
                    last.then_inc(s_R3a_ready, 1)
                if u == 2 and l2:
                    pe.wait_ge(s_OP_out, i - 1)
                    for j in range(2):
                        last = mm(BANK["R3b"][:, j * TG:(j + 1) * TG], W(W_1 + 2 + j), t2T[:], start=True, stop=True)
                    last.then_inc(s_R3b_ready, 1)
                if u == 3 and l2:
                    pe.wait_ge(s_R3a_out, 2 * (i - 1))
                    pe.wait_ge(s_R3b_out, 2 * (i - 1))
                    for b in range(GB):
                        for j in range(NJ):
                            last = mm(BANK["R4"][:, b * D:(b + 1) * D], hT[:, j, b * S:(b + 1) * S], W(W_2 + j),
                                      start=(j == 0), stop=(j == NJ - 1))
                    last.then_inc(s_R4_ready, 1)
                if u == 4 and B is not None:
                    if l2:
                        pe.wait_ge(s_R3b_out, 2 * (i - 1))
                    elif Lp is not None:
                        if above_zero(i - 1):
                            pe.wait_ge(s_OP_out, i - 1)
                    jobs = ((cT, W_V1),) if B else ((tT, W_V), (cT, W_G))
                    for k, (t, w) in enumerate(jobs):
                        for b in range(GB):
                            at = (k * GB + b) * D
                            last = mm(BANK["V"][:, at:at + D], t[:, b * S:(b + 1) * S], W(w), start=True, stop=True)
                    last.then_inc(s_V_ready, 1)
                if u == 5 and l2:
                    pe.wait_ge(s_x3, i - 1)
                    transpose_group(BANK["R5"], x3).then_inc(s_R5_ready, 1)
                if u == 5 and A == 0:
                    if B is not None:
                        pe.wait_ge(s_v_aug, i + 2)
                        pe.wait_ge(s_xg, i + 2)
                    pe.wait_ge(s_xn, i + 3)
                    transpose_group(BANK["P1"], flat(xn))
                    pe.wait_ge(s_c_in, 16 * (i + 3))
                    transpose_group(BANK["P1"][:, TG:2 * TG], flat(c_in)).then_inc(s_P1_ready, 1)
                if u == 6 and A is not None:
                    if l2:
                        pe.wait_ge(s_R5_out, i - 1)
                    else:
                        if A == 1:
                            pe.wait_ge(s_R5_out, NG)
                        if above_zero(i + 2):
                            for kind in "kq":
                                pe.wait_ge(s_first[kind], 2 * (i + 2))
                    if A == 0:
                        pe.wait_ge(s_P1_out, 2 * (i + 3))
                        src_k, src_q = tT[:], tT[:]
                    else:
                        pe.wait_ge(s_c_back, i + 3 - NG)
                        src_k, src_q = cT[:], x3T_of(i + 2 - NG)
                    mm(BANK["QK"][:, 0:TG], W(W_K1 if A else W_K), src_k, start=True, stop=True)
                    mm(BANK["QK"][:, TG:2 * TG], W(W_Q1 if A else W_Q), src_q, start=True, stop=True).then_inc(s_QK_ready, 1)
                if u == 6 and Lp is not None:
                    if A != 0 and B is not None:
                        pe.wait_ge(s_v_aug, i + 2)
                        if B == 0:
                            pe.wait_ge(s_xg, i + 2)
                    elif B is None:
                        pe.wait_ge(s_OP_out, i - 1)
                    pe.wait_ge(s_aT, GB * i)
                    for b in range(GB):
                        last = mm(BANK["OP"][:, b * D:(b + 1) * D], aT[:, b], W(W_O1 if Lp else W_O), start=True, stop=True)
                    last.then_inc(s_OP_ready, 1)

            def body(i, L, Lp, A, B, l2, par=None):
                par = parity(i, par)
                for u in range(NU):
                    if L is not None:
                        scores(i, u, par)
                    if u >= LT and L is not None:
                        turn(i, u - LT)
                    elif u < LT and Lp is not None:
                        turn(i - 1, u - LT + NU)
                    if u >= LP and L is not None:
                        values(i, u - LP, par)
                    elif u < LP and Lp is not None:
                        values(i - 1, u - LP + NU, 1 - par)
                    if Lp is not None and u in (0, 4):
                        o_turn(i - 1, u // 4)
                    if Lp is not None and u in (1, 5):
                        o_back(i - 1, u // 4)
                    side(i, u, L, Lp, A, B, l2)

            schedule(pe, body)

        @block.scalar
        def _(act):
            A = nc.scalar.activation
            for r, v, k in ((BQ, bq, 1), (BK, bk, 1), (BV, bv, 1), (G1, g1, 1), (BE1, be1, 1), (G2, g2, 1),
                            (BE2, be2, 1), (B1, b1, NJ), (BQ1, bqkv1, 3)):
                act.dma_start(vec_rows[r:r + k], row(v)).then_inc(s_vec_rows, 16)
            for r, v in enumerate((bo, bg, b2, bo1, gam, bet)):
                act.dma_start(rep[:, r], row(v).to_broadcast([128, 128])).then_inc(s_rep, 16)

            act.wait_ge(s_w_T, 1)
            for n in (W_Q, W_K):
                A(W(n).rearrange("p (d h) -> p d h", d=HD),
                  wbanks[0][:, n * 128:(n + 1) * 128].rearrange("p (h d) -> p d h", d=HD), ACT.Copy)
            A(W(2, 2), wbanks[0][:, 256:512], ACT.Copy).then_inc(s_w_sb, 1)
            for c in (1, 2):
                act.wait_ge(s_w_T, c + 1)
                A(W(4 * c, 4), wbanks[c][:, :], ACT.Copy).then_inc(s_w_sb, 1)
            act.wait_ge(s_vecs, 2)
            act.wait_ge(s_ones, 2)

            def exps(i, u):
                act.wait_ge(s_turned, NU * i + u + 1)
                if above_zero(NU * i + u + 1 - RP):
                    act.wait_ge(s_values, NU * i + u + 1 - RP)
                A(p_sb[:, u % RP], E_ps[u % 2][:, :], ACT.Exp).then_inc(s_exps, 1)

            def o_out(i, b):
                act.wait_ge(s_values, NU * i + UB * (b + 1))
                A(oT_aug[:], O_ps[:, :], ACT.Copy).then_inc(s_o_out, 1)

            def a_out(i, b, L):
                act.wait_ge(s_o_back, GB * i + b + 1)
                bias = vec[:, BV1:BV1 + 1] if L else vec[:, BV:BV + 1]
                A(aT[:, b], N_ps[:, 0:128], ACT.Identity, bias=bias).then_inc(s_aT, 1)

            def v_out(i, par):
                act.wait_ge(s_V_ready, i + 1)
                if above_zero(NU * (i - 1)):
                    act.wait_ge(s_values, NU * (i - 1))
                A(v_aug[:, par, :, :, 0:HD].rearrange("p b h d -> p (b h) d"),
                  BANK["V"][:, 0:TG].rearrange("p (n d) -> p n d", d=HD), ACT.Copy).then_inc(s_v_aug, 1)

            def split_first(kind, grp, src, bias, scale):
                act.wait_ge(s_QK_ready, grp + 1)
                if above_zero(grp):
                    act.wait_ge(s_stack[kind], STACKED * grp)
                A(parts[kind][:, 0], src, ACT.Identity, bias=bias, scale=scale).then_inc(s_first[kind], 1)
                A(full[kind][:], src, ACT.Identity, bias=bias, scale=scale).then_inc(s_first[kind], 1)

            def split_second(kind, grp):
                act.wait_ge(s_resid[kind], grp + 1)
                A(parts[kind][:, 1], resid[kind][:], ACT.Copy).then_inc(s_part2[kind], 1)

            col = lambda t, n: t[:, n:n + 1]

            def side(i, u, L, Lp, Ab, B, l2, par):
                if u == 0 and l2:
                    act.wait_ge(s_R2_ready, i - 1)
                    A(t2T[:], BANK["R2"][:, 0:TG], ACT.Identity, bias=col(vec, BE2), scale=col(vec, G2)).then_inc(s_R2_out, 1)
                if u == 1 and l2:
                    act.wait_ge(s_R3a_ready, i - 1)
                    for j in range(2):
                        A(hT[:, j], BANK["R3a"][:, j * TG:(j + 1) * TG], ACT.Relu, bias=col(vec, B1 + j)).then_inc(s_R3a_out, 1)
                if u == 4 and B is not None:
                    v_out(i + 1, 1 - par)
                if u == 5 and l2:
                    act.wait_ge(s_R5_ready, i - 1)
                    A(x3T_of(i - 2), BANK["R5"][:, 0:TG], ACT.Copy).then_inc(s_R5_out, 1)
                if u == 5 and Ab == 0:
                    act.wait_ge(s_P1_ready, i + 3)
                    if above_zero(i + 2):
                        act.wait_ge(s_c_kept, i + 2)
                    A(tT[:], BANK["P1"][:, 0:TG], ACT.Identity, bias=col(vec, BE1), scale=col(vec, G1)).then_inc(s_P1_out, 1)
                    A(cT[:], BANK["P1"][:, TG:2 * TG], ACT.Copy).then_inc(s_P1_out, 1)
                if u == 6 and Ab is not None:
                    split_first("k", i + 2, BANK["QK"][:, 0:TG], col(vec_p, BK1 if Ab else BK), 1.0)
                    split_first("q", i + 2, BANK["QK"][:, TG:2 * TG], col(vec_ps, BQ1 if Ab else BQ), SCALE)
                if u == 7 and Ab is not None:
                    split_second("k", i + 2)
                    split_second("q", i + 2)

            def body(i, L, Lp, Ab, B, l2, par=None):
                par = parity(i, par)
                for u in range(NU):
                    if u >= LT and L is not None:
                        exps(i, u - LT)
                    elif u < LT and Lp is not None:
                        exps(i - 1, u - LT + NU)
                    if Lp is not None and u == 3:
                        o_out(i - 1, 1)
                    if L is not None and u == 7:
                        o_out(i, 0)
                    if Lp is not None and u in (1, 5):
                        a_out(i - 1, u // 4, Lp)
                    side(i, u, L, Lp, Ab, B, l2, par)

            schedule(act, body)

        @block.vector
        def _(dve):
            V = nc.vector
            for par in range(2):
                V.memset(q_st[:, par], 0.0).then_inc(s_zeroed, 1)
            dve.wait_ge(s_vec_rows, 16 * 9)
            V.tensor_copy(vec_rows_p[:, :].rearrange("r (d h) -> r d h", d=HD),
                          vec_rows[:, :].rearrange("r (h d) -> r d h", d=HD)).then_inc(s_rows_p, 1)
            dve.wait_ge(s_vec_T, 1)
            V.tensor_copy(vec[:], N_ps[:, 0:NVEC])
            V.tensor_copy(vec_p[:], N_ps[:, 32:32 + NVEC]).then_inc(s_vecs, 1)
            dve.wait_ge(s_vecs, 1)
            V.tensor_scalar(vec_ps[:], vec_p[:], SCALE, None, ALU.mult).then_inc(s_vecs, 1)
            dve.wait_ge(s_w_T, 4)
            V.tensor_copy(W(12), wbanks[3][:, 0:128])
            for n in (W_Q1, W_K1):
                V.tensor_copy(W(n).rearrange("p (d h) -> p d h", d=HD),
                              wbanks[3][:, (n - 12) * 128:(n - 11) * 128].rearrange("p (h d) -> p d h", d=HD))
            V.tensor_copy(W(15), wbanks[3][:, 384:512]).then_inc(s_w_sb, 1)
            dve.wait_ge(s_w_T, 5)
            V.tensor_copy(W(16), wbanks[4][:, 0:128]).then_inc(s_w_sb, 1)
            dve.wait_ge(s_vecs, 2)

            def mask_bias(grp, b):
                dve.wait_ge(s_m_in[b], 16 * (grp + 1))
                V.tensor_scalar(mbias[:, b], m_in[:, b], -1.0, BIG, ALU.add, ALU.mult).then_inc(s_mbias[b], 1)

            def masked_max(i, u, L):
                b = u // UB
                dve.wait_ge(s_scores, NU * i + u + 1)
                if above_zero(NU * i + u + 1 - RT):
                    dve.wait_ge(s_turned, NU * i + u + 1 - RT)
                if L == 0 and u % UB == 0:
                    dve.wait_ge(s_mbias[b], i + 1)
                settled(dve, i)
                for j in range(UH):
                    t, s, m = t_sb[:, u % RT, j], S_ps[u % 2][:, j * S:(j + 1) * S], mx[:, u % RT, j:j + 1]
                    if L == 0:
                        last = V.tensor_tensor_reduce(t, s, mbias[:, b], 1.0, -3.4e38, ALU.add, ALU.max, m)
                    else:
                        last = V.tensor_scalar(t, s, 1.0, None, ALU.mult, ALU.max, accum_out=m)
                last.then_inc(s_masked, 1)

            def normalise(i, b):
                dve.wait_ge(s_o_turned, GB * i + b + 1)
                nv = N_ps[:, :].rearrange("p (h w) -> p h w", w=VW)
                V.reciprocal(rden[:], nv[:, :, HD]).then_inc(s_rden, 1)
                dve.wait_ge(s_rden, GB * i + b + 1)
                V.tensor_tensor(o_n[:, :, :], nv[:, :, 0:HD], rden[:].unsqueeze(2).to_broadcast([128, NH, HD]),
                                ALU.mult).then_inc(s_o_n, 1)

            def norm_stats(k, src, n):
                for b in range(GB):
                    last = V.bn_stats(stats[k][:, b], src[:, b * D:(b + 1) * D])
                last.then_inc(s_ln[k], 1)
                dve.wait_ge(s_ln[k], 2 * n + 1)
                settled(dve, n)
                for b in range(GB):
                    last = V.bn_aggr(mv[k][:, b], stats[k][:, b])
                last.then_inc(s_ln[k], 1)

            def norm_apply(k, dst, src, n, done):
                dve.wait_ge(s_rstd[k], n + 1)
                for b in range(GB):
                    last = V.tensor_scalar(dst[:, b], src[:, b * D:(b + 1) * D], mv[k][:, b, 0:1], rstd[k][:, b:b + 1],
                                           ALU.subtract, ALU.mult)
                last.then_inc(done, 1)

            def split_resid(kind, grp):
                dve.wait_ge(s_first[kind], 2 * (grp + 1))
                V.tensor_tensor(resid[kind][:], full[kind][:], parts[kind][:, 0], ALU.subtract).then_inc(s_resid[kind], 1)

            def split_third(kind, grp):
                dve.wait_ge(s_part2[kind], grp + 1)
                V.tensor_tensor(parts[kind][:, 2], resid[kind][:], parts[kind][:, 1], ALU.subtract).then_inc(s_part3[kind], 1)

            def side(i, u, L, Lp, A, B, l2):
                if L == 0 and u == 1:
                    mask_bias(i, 1)
                if B == 0 and u == 5:
                    mask_bias(i + 1, 0)
                if u == 0 and B is not None:
                    split_third("k", i + 1)
                    split_third("q", i + 1)
                if u == 2 and l2:
                    dve.wait_ge(s_R3b_ready, i - 1)
                    for j in range(2):
                        V.tensor_scalar(hT[:, 2 + j], BANK["R3b"][:, j * TG:(j + 1) * TG], vec[:, B1 + 2 + j:B1 + 3 + j], 0.0,
                                        ALU.add, ALU.max).then_inc(s_R3b_out, 1)
                if u == 3 and A == 0:
                    dve.wait_ge(s_x_in, 16 * (i + 3))
                    norm_stats("a", flat(x_in), i + 2)
                if u == 3 and l2:
                    dve.wait_ge(s_R4_ready, i - 1)
                    dve.wait_ge(s_x2b, i - 1)
                    V.tensor_tensor(x3[:], BANK["R4"][:, 0:TG], x2b[:], ALU.add).then_inc(s_x3, 1)
                if u == 4 and B == 0:
                    dve.wait_ge(s_v_aug, i + 2)
                    dve.wait_ge(s_V_ready, i + 2)
                    dve.wait_ge(s_xb, i + 2)
                    V.tensor_tensor(xg_all[:, bass.ts(i + 1, TG)], BANK["V"][:, TG:2 * TG], xb[:], ALU.add).then_inc(s_xg, 1)
                if u == 4 and A == 0:
                    if above_zero(i + 2):
                        dve.wait_ge(s_P1_ready, i + 2)
                    norm_apply("a", xn, flat(x_in), i + 2, s_xn)
                if u == 5 and A == 1:
                    dve.wait_ge(s_V_ready, i + 2)
                    dve.wait_ge(s_c_kept, NG)
                    V.tensor_copy(cT[:], cT_all[:, bass.ts(i + 2 - NG, TG)]).then_inc(s_c_back, 1)
                if u == 6 and Lp is not None:
                    dve.wait_ge(s_OP_ready, i)
                    if Lp == 0:
                        if above_zero(i - 1):
                            dve.wait_ge(s_x2b, i - 1)
                        dve.wait_ge(s_xg, i)
                        res = xg_all[:, bass.ts(i - 1, TG)]
                    else:
                        dve.wait_ge(s_x2b, NG)
                        dve.wait_ge(s_x3b, NG)
                        res = x3b_all[:, bass.ts(i - 1 - NG, TG)]
                    V.tensor_tensor(x2[:], BANK["OP"][:, 0:TG], res, ALU.add).then_inc(s_OP_out, 1)
                    dve.wait_ge(s_OP_out, i)
                    norm_stats("b", x2, i - 1)
                if u == 6 and A == 0:
                    dve.wait_ge(s_P1_out, 2 * (i + 3))
                    V.tensor_copy(cT_all[:, bass.ts(i + 2, TG)], cT[:]).then_inc(s_c_kept, 1)
                if u == 7 and A is not None:
                    split_resid("k", i + 2)
                    split_resid("q", i + 2)
                if u == 7 and Lp is not None:
                    if Lp == 0:
                        if above_zero(i - 1):
                            dve.wait_ge(s_R2_ready, i - 1)
                    else:
                        dve.wait_ge(s_R2_ready, NG)
                        if above_zero(i - 1 - NG):
                            dve.wait_ge(s_yg, i - 1 - NG)
                    norm_apply("b", xn2, x2, i - 1, s_xn2)

            def body(i, L, Lp, A, B, l2, par=None):
                for u in range(NU):
                    if L is not None:
                        masked_max(i, u, L)
                    if Lp is not None and u in (0, 4):
                        normalise(i - 1, u // 4)
                    side(i, u, L, Lp, A, B, l2)

            schedule(dve, body)

        @block.gpsimd
        def _(pool):
            G = nc.gpsimd
            G.memset(ident[:], 0.0).then_inc(s_ident, 1)
            pool.wait_ge(s_ident, 1)
            G.affine_select(out=ident[:], in_=ident[:], compare_op=ALU.not_equal, fill=1.0, base=0, pattern=[[-1, 128]],
                            channel_multiplier=1).then_inc(s_ident, 1)
            G.memset(expo[:], -0.5)
            for par in range(2):
                G.memset(k_st[:, par], 0.0).then_inc(s_zeroed, 1)
                G.memset(v_aug[:, par], 1.0).then_inc(s_ones, 1)
            pool.wait_ge(s_rep, 16 * NREP)
            G.tensor_tensor(bias_og[:], rep[:, R_BO], rep[:, R_BG], ALU.add).then_inc(s_bias_og, 1)
            pool.wait_ge(s_bias_og, 1)
            pool.wait_ge(s_ones, 2)
            per_row = lambda t: t.unsqueeze(1).to_broadcast([128, GB, D])
            grouped = lambda t: t.rearrange("p (b d) -> p b d", b=GB)

            def shift(i, u):
                pool.wait_ge(s_masked, NU * i + u + 1)
                t = t_sb[:, u % RT]
                G.tensor_tensor(t, t, mx[:, u % RT].unsqueeze(2).to_broadcast([128, UH, S]), ALU.subtract).then_inc(s_shifted, 1)

            def inverse_root(k, n):
                pool.wait_ge(s_ln[k], 2 * n + 2)
                settled(pool, n)
                G.tensor_scalar(ve[k][:], mv[k][:, :, 1], EPS, None, ALU.add).then_inc(s_ve[k], 1)
                pool.wait_ge(s_ve[k], n + 1)
                G.tensor_tensor(rstd[k][:], ve[k][:], expo[:], ALU.pow).then_inc(s_rstd[k], 1)

            def body(i, L, Lp, A, B, l2, par=None):
                for u in range(NU):
                    if L is not None:
                        shift(i, u)
                    if u == 3 and A == 0:
                        inverse_root("a", i + 2)
                    if u == 4 and l2:
                        pool.wait_ge(s_x3, i - 1)
                        G.tensor_tensor(grouped(x3b_all[:, bass.ts(i - 2, TG)]), grouped(x3[:]), per_row(rep[:, R_BO1]),
                                        ALU.add).then_inc(s_x3b, 1)
                    if u == 5 and A == 0:
                        pool.wait_ge(s_x_in, 16 * (i + 3))
                        if above_zero(i + 2):
                            pool.wait_ge(s_xg, i + 2)
                        G.tensor_tensor(grouped(xb[:]), x_in[:, :, :], per_row(bias_og[:]), ALU.add).then_inc(s_xb, 1)
                    if u == 6 and Lp is not None:
                        inverse_root("b", i - 1)
                    if u == 7 and Lp == 0:
                        pool.wait_ge(s_OP_out, i)
                        if above_zero(i - 1):
                            pool.wait_ge(s_x3, i - 1)
                        G.tensor_tensor(grouped(x2b[:]), grouped(x2[:]), per_row(rep[:, R_B2]), ALU.add).then_inc(s_x2b, 1)
                    if u == 7 and Lp == 1:
                        pool.wait_ge(s_xn2, i)
                        G.tensor_tensor(yg[:, :, :], xn2[:, :, :], per_row(rep[:, R_GAM]), ALU.mult).then_inc(s_yg, 1)
                        pool.wait_ge(s_yg, i - NG)
                        if above_zero(16 * (i - 1 - NG)):
                            pool.wait_ge(s_stored, 16 * (i - 1 - NG))
                        G.tensor_tensor(y_out[:, :, :], yg[:, :, :], per_row(rep[:, R_BET]), ALU.add).then_inc(s_y_out, 1)

            schedule(pool, body)


_INS = ["x", "ctx_1024", "mask_BxSxS2_fk0", "L0_xattn_Wq", "L0_xattn_bq", "L0_xattn_Wk", "L0_xattn_bk", "L0_xattn_Wv",
        "L0_xattn_bv", "L0_xattn_Wo", "L0_xattn_bo", "L0_xattn_Wg", "L0_xattn_bg", "L0_xattn_W1", "L0_xattn_b1",
        "L0_xattn_W2", "L0_xattn_b2", "L0_xattn_g1", "L0_xattn_be1", "L0_xattn_g2", "L0_xattn_be2", "L1_xattn_W_qkv",
        "L1_xattn_b_qkv", "L1_xattn_W_o", "L1_xattn_b_o", "L1_xattn_ln_gamma", "L1_xattn_ln_beta"]
_OUTS = [((NB, S, D), "float32")]


def kernel(**inputs):
    import numpy as _np
    import concourse.bacc as _bacc
    from concourse import mybir as _mybir
    from concourse.bass_utils import run_bass_kernel_spmd as _run

    nc = _bacc.Bacc("TRN2", target_bir_lowering=False, num_devices=1)
    arrays, args = {}, []
    for name in _INS:
        a = _np.ascontiguousarray(inputs[name])
        arrays[f"in_{name}_dram"] = a
        args.append(nc.dram_tensor(f"in_{name}_dram", a.shape, _mybir.dt.from_np(a.dtype), kind="ExternalInput").ap())
    for n, (shape, dtype) in enumerate(_OUTS):
        dt = _mybir.dt.from_np(_np.dtype(dtype))
        args.append(nc.dram_tensor(f"out_{n}_dram", shape, dt, kind="ExternalOutput").ap())
    build(nc, *args)
    r = _run(nc, [arrays], core_ids=[0])
    return tuple(r.results[0][f"out_{n}_dram"] for n in range(len(_OUTS)))[0]
```

```python
import concourse.bass as bass
from concourse import mybir
from contextlib import ExitStack

F32 = mybir.dt.float32
BF16 = mybir.dt.bfloat16
ALU = mybir.AluOpType
ACT = mybir.ActivationFunctionType

NB, S, D = 16, 128, 128
NH, HD, FF = 16, 8, 512
GB = 2
NG = NB // GB
TG = GB * S
UH = 4
UB = NH // UH
NU = GB * UB
NJ = FF // 128
NP = 3
NT = NH // 2
OW = HD + 1
VW = 32
SCALE = HD ** -0.5
EPS = 1e-5
BIG = 1.0e9
LT, LP = 3, 4
RT, RP = 4, 4
ROWS = NP * HD * NP
SPREAD = {"k": 1, "q": NP - 1}

BQ, BK, BV, G1, BE1, G2, BE2, B1, BQ1, BK1, BV1 = 0, 1, 2, 3, 4, 5, 6, 7, 11, 12, 13
NVEC, VECS_ACT, VECS_POOL = 14, 6, 3
R_BO, R_BG, R_B2, R_BO1, R_GAM, R_BET, NREP = 0, 1, 2, 3, 4, 5, 6
W_Q, W_K, W_V, W_G, W_O, W_1, W_2, W_Q1, W_K1, W_V1, W_O1, NW = 0, 1, 2, 3, 4, 5, 9, 13, 14, 15, 16, 17


def build(nc, x, ctx_, mask, Wq, bq, Wk, bk, Wv, bv, Wo, bo, Wg, bg, W1, b1, W2, b2, g1, be1, g2, be2,
          Wqkv1, bqkv1, Wo1, bo1, gam, bet, out):
    x_v = x.rearrange("(g b) s d -> g s b d", b=GB)
    c_v = ctx_.rearrange("(g b) s d -> g s b d", b=GB)
    o_v = out.rearrange("(g b) s d -> g s b d", b=GB)
    row = lambda a: a.rearrange("(r n) -> r n", n=128)

    with ExitStack() as es:
        sb = lambda name, shape, dt=F32: es.enter_context(nc.sbuf_tensor(name, shape, dt))
        ps = lambda name: es.enter_context(nc.psum_tensor(name, [128, 512], F32))

        def above_zero(count):
            return not isinstance(count, int) or count > 0

        def body_is(i, n):
            return isinstance(i, int) and i == n

        def settled(eng, i):
            if not isinstance(i, int):
                eng.sem_inc(s_settled[eng.engine.name], 1)

        sem = lambda name: es.enter_context(nc.semaphore(name))
        s_w_first, s_w_rest = sem("first_weights_loaded"), sem("other_weights_loaded")
        s_vec_rows, s_rep = sem("vec_rows_loaded"), sem("rep_loaded")
        s_vec_rows_pool = sem("vec_rows_loaded_by_GpSimd_queue")
        s_ident, s_ones = sem("ident_made"), sem("ones_set")
        s_zeroed = [sem(f"stacks_zeroed{par}") for par in range(2)]
        s_rows_p, s_vec_T, s_vecs = sem("rows_permuted"), sem("vectors_turned"), sem("vectors_in_sbuf")
        s_w_T, s_w_sb, s_bias_og = sem("weights_turned"), sem("weights_in_sbuf"), sem("bias_og_made")
        s_x_in, s_c_in, s_stored = sem("x_loaded"), sem("context_loaded"), sem("y_stored")
        s_m_in = [sem(f"mask_loaded{b}") for b in range(GB)]
        s_scores, s_masked, s_shifted = sem("scores_ready"), sem("masked_and_max"), sem("max_subtracted")
        s_turned, s_exps, s_values = sem("scores_turned"), sem("exps_ready"), sem("values_summed")
        s_o_out, s_o_turned, s_rden = sem("o_in_sbuf"), sem("o_turned"), sem("sums_inverted")
        s_o_n, s_o_back, s_aT, s_v_aug = sem("o_normalised"), sem("o_turned_back"), sem("aT_in_sbuf"), sem("v_in_place")
        s_mbias = [sem(f"mask_bias{b}") for b in range(GB)]
        by_kind = lambda name: {k: sem(f"{name}_{k}") for k in "kq"}
        s_first, s_resid, s_part2 = by_kind("split1"), by_kind("resid"), by_kind("split2")
        s_part3 = by_kind("split3")
        s_placed = by_kind("placed")
        s_stack = {k: [sem(f"stacked_{k}{par}") for par in range(2)] for k in "kq"}
        by_norm = lambda name: {k: sem(f"{name}_{k}") for k in "ab"}
        s_ln, s_ve, s_rstd = by_norm("norm_stats"), by_norm("norm_var"), by_norm("norm_rstd")
        s_P1_ready, s_P1_out = sem("P1_ready"), sem("P1_out")
        s_QK_ready, s_V_ready = sem("QK_ready"), sem("V_ready")
        s_c_kept, s_c_back = sem("context_kept"), sem("context_back")
        s_R2_ready, s_R2_out = sem("R2_ready"), sem("R2_out")
        s_R3a_ready, s_R3a_out = sem("R3a_ready"), sem("R3a_out")
        s_R3b_ready, s_R3b_out = sem("R3b_ready"), sem("R3b_out")
        s_R4_ready, s_R5_ready, s_R5_out = sem("R4_ready"), sem("R5_ready"), sem("R5_out")
        s_OP_ready, s_OP_out = sem("OP_ready"), sem("OP_out")
        s_xn, s_xb, s_xg, s_xn2 = sem("xn_made"), sem("xb_made"), sem("xg_made"), sem("xn2_made")
        s_x2b, s_x3, s_x3b, s_yg, s_y_out = sem("x2b_made"), sem("x3_made"), sem("x3b_made"), sem("yg_made"), sem("y_made")
        s_settled = {e: sem(f"settled_{e}") for e in ("SP", "DVE", "Pool")}

        ident = sb("ident", [128, 128])
        wraw = sb("wraw", [128, NW * 128])
        wT = sb("wT", [128, NW * 128])
        vec_rows = sb("vec_rows", [NVEC, 128])
        vec_rows_p = sb("vec_rows_p", [NVEC, 128])
        vec = sb("vec", [128, NVEC])
        vec_p = sb("vec_p", [128, NVEC])
        rep = sb("rep", [128, NREP, 128])
        bias_og = sb("bias_og", [128, 128])
        table = sb("table", [128, 1])
        expo = sb("expo", [128, GB])
        W = lambda n, k=1: wT[:, n * 128:(n + k) * 128]
        x_in = sb("x_in", [128, GB, D])
        c_in = sb("c_in", [128, GB, D])
        m_in = sb("m_in", [128, GB, S])
        mbias = sb("mbias", [128, GB, S])
        xg_all = sb("xg_all", [128, NG * TG])
        x3b_all = sb("x3b_all", [128, NG * TG])
        xn = sb("xn", [128, GB, D])
        xb = sb("xb", [128, TG])
        tT = sb("tT", [128, TG])
        cT = sb("cT", [128, TG])
        cT_all = sb("cT_all", [128, NG * TG])
        x3T_all = sb("x3T_all", [128, NG * TG])
        resid = {k: sb(f"resid_{k}", [128, TG]) for k in "kq"}
        parts = {k: sb(f"parts_{k}", [128, 2, NP, TG], BF16) for k in "kq"}
        q_st = sb("q_st", [128, 2, NH, TG], BF16)
        k_st = sb("k_st", [128, 2, NH, TG], BF16)
        k_rows = sb("k_rows", [NP * HD, NH, TG], BF16)
        v_aug = sb("v_aug", [128, 2, GB, NT, 2, VW + OW])
        t_sb = sb("t_sb", [128, RT, UH, S])
        mx = sb("mx", [128, RT, UH])
        p_sb = sb("p_sb", [128, RP, UH * S])
        oT_aug = sb("oT_aug", [128, NT * VW])
        rden = sb("rden", [128, NH])
        o_n = sb("o_n", [128, NH, HD])
        aT = sb("aT", [128, GB, S])
        stats = {k: sb(f"stats_{k}", [128, GB, 6]) for k in "ab"}
        mv = {k: sb(f"mv_{k}", [128, GB, 2]) for k in "ab"}
        ve = {k: sb(f"ve_{k}", [128, GB]) for k in "ab"}
        rstd = {k: sb(f"rstd_{k}", [128, GB]) for k in "ab"}
        x2 = sb("x2", [128, TG])
        x2b = sb("x2b", [128, TG])
        xn2 = sb("xn2", [128, GB, D])
        t2T = sb("t2T", [128, TG])
        hT = sb("hT", [128, NJ, TG])
        x3 = sb("x3", [128, TG])
        yg = sb("yg", [128, GB, D])
        y_out = sb("y_out", [128, GB, D])

        S_ps = [ps("S0"), ps("S1")]
        E_ps = [ps("E0"), ps("E1")]
        O_ps = [ps("O0"), ps("O1")]
        D_ps = [ps("D0"), ps("D1")]
        BANK = {"R3a": 0, "R4": 0, "P1": 0, "QK": 0,
                "R2": 1, "R3b": 1, "V": 1, "R5": 1, "OP": 1}
        BANK = {job: D_ps[n] for job, n in BANK.items()}
        wbanks = [D_ps[1], S_ps[0], S_ps[1], E_ps[0], E_ps[1]]

        block = es.enter_context(nc.Block())

        def schedule(eng, body):
            body(-2, None, None, 0, None, False)
            body(-1, None, None, 0, 0, False)
            body(0, 0, None, 0, 0, False)
            body(1, 0, 0, 0, 0, False)
            with eng.Fori(1, (NG - 2) // 2) as pair:
                i = 2 * pair
                body(i, 0, 0, 0, 0, True, 0)
                body(i + 1, 0, 0, 0, 0, True, 1)
            body(NG - 2, 0, 0, 1, 0, True)
            body(NG - 1, 0, 0, 1, 1, True)
            body(NG, 1, 0, 1, 1, True)
            body(NG + 1, 1, 1, 1, 1, True)
            with eng.Fori((NG + 2) // 2, (2 * NG - 2) // 2) as pair:
                i = 2 * pair
                body(i, 1, 1, 1, 1, False, 0)
                body(i + 1, 1, 1, 1, 1, False, 1)
            body(2 * NG - 2, 1, 1, None, 1, False)
            body(2 * NG - 1, 1, 1, None, None, False)
            body(2 * NG, None, 1, None, None, False)

        def parity(i, par):
            return i % 2 if par is None else par

        def stacked(kind, g, par):
            return 8 * SPREAD[kind] * (g - par) + 16 * SPREAD[kind]

        def qk_slot(A, l2):
            return 1 if A == 1 and not l2 else 6

        def head(c, j):
            return 2 * (c // 2 * UH + j) + c % 2

        flat = lambda t: t[:, :, :].rearrange("p b d -> p (b d)")
        per_row = lambda t: t.unsqueeze(1).to_broadcast([128, GB, D])
        col = lambda t, n: t[:, n:n + 1]
        cT_of = lambda g: cT_all[:, bass.ts(g, TG)]
        x3T_of = lambda g: x3T_all[:, bass.ts(g, TG)]

        @block.sync
        def _(sp):
            def stack(i, par):
                par = parity(i, par)
                k_to, q_to = k_st[:, par], q_st[:, par]
                if above_zero(NU * (i - 1)):
                    sp.wait_ge(s_scores, NU * (i - 1))
                    settled(sp, i)
                if above_zero(i):
                    sp.wait_ge(s_stack["k"][1 - par], stacked("k", i - 1, 1 - par))
                settled(sp, i)
                if not above_zero(i - 1):
                    sp.wait_ge(s_zeroed[i % 2], 2)
                for part, ready in enumerate((s_first, s_part2, s_part3)):
                    for kind, rows in (("k", k_rows[part * HD:(part + 1) * HD]), ("q", q_to[part:NP * HD:NP])):
                        sp.wait_ge(ready[kind], i + 1)
                        settled(sp, i)
                        sp.dma_start(rows, parts[kind][:, par, part]).then_inc(s_placed[kind], 16)
                sp.wait_ge(s_placed["k"], 16 * NP * (i + 1))
                settled(sp, i)
                each = k_rows[:].rearrange("p h s -> p (h s)").unsqueeze(1).to_broadcast([NP * HD, NP, NH * TG])
                sp.dma_start(k_to[0:ROWS], each).then_inc(s_stack["k"][par], 16)
                sp.wait_ge(s_placed["q"], 16 * NP * (i + 1))
                settled(sp, i)
                for r in range(1, NP):
                    sp.dma_start(q_to[r * NP * HD:(r + 1) * NP * HD], q_to[0:NP * HD]).then_inc(s_stack["q"][par], 16)

            def load_weight(w, n, k, done):
                dst = wraw[:, n * 128:(n + k) * 128].rearrange("p (j n) -> p j n", j=k)
                sp.dma_start(dst, w.rearrange("(j p) n -> p j n", p=128)).then_inc(done, 16)

            sp.dma_start(x_in[:], x_v[0]).then_inc(s_x_in, 16)
            for w, n in ((Wk, W_K), (Wq, W_Q), (Wv, W_V), (Wg, W_G)):
                load_weight(w, n, 1, s_w_first)
            sp.dma_start(c_in[:], c_v[0]).then_inc(s_c_in, 16)
            for b in range(GB):
                sp.dma_start(m_in[:, b], mask[b]).then_inc(s_m_in[b], 16)
            for r, v in enumerate((bo, bg, b2, bo1, gam, bet)):
                sp.dma_start(rep[:, r], row(v).to_broadcast([128, 128])).then_inc(s_rep, 16)
            for w, n, k in ((Wqkv1, W_Q1, 3), (Wo, W_O, 1), (W1, W_1, NJ), (Wo1, W_O1, 1)):
                load_weight(w, n, k, s_w_rest)
            sp.dma_start(wraw[:, W_2 * 128:(W_2 + NJ) * 128], W2).then_inc(s_w_rest, 16)

            def inputs(i):
                sp.wait_ge(s_xb, i)
                settled(sp, i)
                sp.wait_ge(s_xn, i)
                settled(sp, i)
                sp.dma_start(x_in[:], x_v[i]).then_inc(s_x_in, 16)
                sp.wait_ge(s_P1_ready, i)
                settled(sp, i)
                sp.dma_start(c_in[:], c_v[i]).then_inc(s_c_in, 16)

            def mask_load(i, b):
                sp.wait_ge(s_mbias[b], i)
                settled(sp, i)
                sp.dma_start(m_in[:, b], mask[GB * i + b]).then_inc(s_m_in[b], 16)

            def store(g):
                sp.wait_ge(s_y_out, g + 1)
                settled(sp, g + 1)
                sp.dma_start(o_v[g], y_out[:]).then_inc(s_stored, 16)

            def body(i, masks, more, stores, stacks, par=None):
                if masks:
                    mask_load(i + 1, 0)
                if stacks:
                    stack(i + 1, None if par is None else 1 - par)
                if masks:
                    mask_load(i + 1, 1)
                if more:
                    inputs(i + 3)
                if stores:
                    store(i - 2 - NG)

            body(-2, False, True, False, False)
            body(-1, False, True, False, True)
            body(0, True, True, False, True)
            body(1, True, True, False, True)
            with sp.Fori(1, (NG - 4) // 2) as pair:
                i = 2 * pair
                body(i, True, True, False, True, 0)
                body(i + 1, True, True, False, True, 1)
            body(NG - 4, True, True, False, True)
            body(NG - 3, True, False, False, True)
            body(NG - 2, True, False, False, True)
            for i in (NG - 1, NG, NG + 1):
                body(i, False, False, False, True)
            with sp.Fori((NG + 2) // 2, (2 * NG - 2) // 2) as pair:
                i = 2 * pair
                body(i, False, False, True, True, 0)
                body(i + 1, False, False, True, True, 1)
            body(2 * NG - 2, False, False, True, True)
            for g in (NG - 3, NG - 2, NG - 1):
                store(g)
            sp.wait_ge(s_stored, 16 * NG)
            settled(sp, 16 * NG)

        @block.tensor
        def _(pe):
            mm, transpose = nc.tensor.matmul, nc.tensor.transpose

            pe.wait_ge(s_ident, 2)

            def weights_T(banks):
                for c in banks:
                    for n in range(4 * c, min(4 * c + 4, NW)):
                        last = transpose(wbanks[c][:, (n % 4) * 128:(n % 4 + 1) * 128], wraw[:, n * 128:(n + 1) * 128], ident[:])
                    last.then_inc(s_w_T, 1)

            pe.wait_ge(s_w_first, 16 * 4)
            weights_T((0,))

            def vectors():
                pe.wait_ge(s_vec_rows, 16 * VECS_ACT)
                pe.wait_ge(s_vec_rows_pool, 16 * VECS_POOL)
                transpose(O_ps[0][:, 0:NVEC], vec_rows[:, :], ident[0:NVEC, 0:NVEC])
                pe.wait_ge(s_rows_p, 1)
                transpose(O_ps[0][:, 32:32 + NVEC], vec_rows_p[:, :], ident[0:NVEC, 0:NVEC]).then_inc(s_vec_T, 1)

            def transpose_group(dst, src):
                for b in range(GB):
                    last = transpose(dst[:, b * 128:(b + 1) * 128], src[:, b * 128:(b + 1) * 128], ident[:])
                return last

            def scores(i, u, par):
                b, c = divmod(u, UB)
                if u == 0:
                    pe.wait_ge(s_stack["k"][par], stacked("k", i, par))
                    pe.wait_ge(s_stack["q"][par], stacked("q", i, par))
                if above_zero(NU * i + u - 1):
                    pe.wait_ge(s_masked, NU * i + u - 1)
                tokens = slice(b * S, (b + 1) * S)
                for j in range(UH):
                    h = head(c, j)
                    last = mm(S_ps[u % 2][:, j * S:(j + 1) * S], q_st[:, par, h, tokens], k_st[:, par, h, tokens],
                              start=True, stop=True)
                last.then_inc(s_scores, 1)

            def turn(i, u):
                pe.wait_ge(s_shifted, NU * i + u + 1)
                if above_zero(NU * i + u - 1):
                    pe.wait_ge(s_exps, NU * i + u - 1)
                for j in range(UH):
                    last = transpose(E_ps[u % 2][:, j * S:(j + 1) * S], t_sb[:, u % RT, j], ident[:])
                last.then_inc(s_turned, 1)

            def values(i, u, par):
                b, c = divmod(u, UB)
                pe.wait_ge(s_exps, NU * i + u + 1)
                if u == 0:
                    pe.wait_ge(s_v_aug, i + 1)
                if c == 0 and above_zero(GB * (i - 1) + b + 1):
                    pe.wait_ge(s_aT, GB * (i - 1) + b + 1)
                x, y = divmod(c, 2)
                for j in range(UH):
                    pair = v_aug[:, par, b, x * UH + j].rearrange("p y e -> p (y e)")
                    last = mm(O_ps[b][VW * j:VW * (j + 1), x * S:(x + 1) * S], pair[:, VW * y:VW * (y + 1)],
                              p_sb[:, u % RP, j * S:(j + 1) * S], start=(y == 0), stop=(y == 1))
                last.then_inc(s_values, 1)

            def o_turn(i, b):
                pe.wait_ge(s_o_out, GB * i + b + 1)
                for c in range(NT * VW // 128):
                    last = transpose(O_ps[b][:, c * 128:(c + 1) * 128], oT_aug[:, c * 128:(c + 1) * 128], ident[:])
                last.then_inc(s_o_turned, 1)

            def o_back(i, b):
                pe.wait_ge(s_o_n, GB * i + b + 1)
                transpose(O_ps[b][:, 0:128], o_n[:, :, :].rearrange("p h d -> p (h d)"), ident[:]).then_inc(s_o_back, 1)

            def project(i, Lp, B, l2):
                if l2:
                    pe.wait_ge(s_R5_out, i - 1)
                elif B is not None:
                    pe.wait_ge(s_v_aug, i + 2)
                    if B == 0:
                        pe.wait_ge(s_xg, i + 2)
                else:
                    pe.wait_ge(s_OP_out, i - 1)
                for b in range(GB):
                    pe.wait_ge(s_aT, GB * (i - 1) + b + 1)
                    last = mm(BANK["OP"][:, b * D:(b + 1) * D], aT[:, b], W(W_O1 if Lp else W_O), start=True, stop=True)
                last.then_inc(s_OP_ready, 1)

            def side(i, u, L, Lp, A, B, l2):
                if u == 0 and l2:
                    pe.wait_ge(s_OP_out, i - 1)
                    pe.wait_ge(s_xn2, i - 1)
                    transpose_group(BANK["R2"], flat(xn2)).then_inc(s_R2_ready, 1)
                if u == 1 and l2:
                    for kind in "kq":
                        pe.wait_ge(s_resid[kind], i + 2)
                    pe.wait_ge(s_R2_out, i - 1)
                    for j in range(2):
                        last = mm(BANK["R3a"][:, j * TG:(j + 1) * TG], W(W_1 + j), t2T[:], start=True, stop=True)
                    last.then_inc(s_R3a_ready, 1)
                if u == 2 and l2:
                    for j in range(2):
                        last = mm(BANK["R3b"][:, j * TG:(j + 1) * TG], W(W_1 + 2 + j), t2T[:], start=True, stop=True)
                    last.then_inc(s_R3b_ready, 1)
                if u == 3 and l2:
                    pe.wait_ge(s_R3a_out, 2 * (i - 1))
                    for b in range(GB):
                        for j in range(NJ):
                            if (b, j) == (0, 2):
                                pe.wait_ge(s_R3b_out, 2 * (i - 1))
                            last = mm(BANK["R4"][:, b * D:(b + 1) * D], hT[:, j, b * S:(b + 1) * S], W(W_2 + j),
                                      start=(j == 0), stop=(j == NJ - 1))
                    last.then_inc(s_R4_ready, 1)
                if u == 4 and B is not None:
                    if l2:
                        pe.wait_ge(s_R3b_out, 2 * (i - 1))
                    elif Lp is not None:
                        if above_zero(i - 1):
                            pe.wait_ge(s_OP_out, i - 1)
                    if B:
                        pe.wait_ge(s_c_back, i + 2 - NG)
                    jobs = ((cT, W_V1),) if B else ((tT, W_V), (cT, W_G))
                    for k, (t, w) in enumerate(jobs):
                        for b in range(GB):
                            at = (k * GB + b) * D
                            last = mm(BANK["V"][:, at:at + D], t[:, b * S:(b + 1) * S], W(w), start=True, stop=True)
                    last.then_inc(s_V_ready, 1)
                if u == 5 and l2:
                    if B is not None:
                        pe.wait_ge(s_v_aug, i + 2)
                        if B == 0:
                            pe.wait_ge(s_xg, i + 2)
                    pe.wait_ge(s_x3, i - 1)
                    transpose_group(BANK["R5"], x3).then_inc(s_R5_ready, 1)
                if u == 5 and A == 0:
                    if l2:
                        pe.wait_ge(s_x3, i - 1)
                    elif above_zero(i + 2):
                        for kind in "kq":
                            pe.wait_ge(s_resid[kind], i + 2)
                    pe.wait_ge(s_xn, i + 3)
                    transpose_group(BANK["P1"], flat(xn))
                    pe.wait_ge(s_c_in, 16 * (i + 3))
                    transpose_group(BANK["P1"][:, TG:2 * TG], flat(c_in)).then_inc(s_P1_ready, 1)
                if u == qk_slot(A, l2) and A is not None:
                    if A == 1 and l2:
                        pe.wait_ge(s_x3, i - 1)
                    elif A == 1:
                        for kind in "kq":
                            pe.wait_ge(s_resid[kind], i + 2)
                    if A == 1:
                        pe.wait_ge(s_R5_out, i + 3 - NG if l2 else NG)
                    if A == 0:
                        pe.wait_ge(s_P1_out, 2 * (i + 3))
                        src_k, src_q = tT[:], tT[:]
                    else:
                        pe.wait_ge(s_c_kept, NG)
                        src_k, src_q = cT_of(i + 2 - NG), x3T_of(i + 2 - NG)
                    mm(BANK["QK"][:, 0:TG], W(W_K1 if A else W_K), src_k, start=True, stop=True)
                    mm(BANK["QK"][:, TG:2 * TG], W(W_Q1 if A else W_Q), src_q, start=True, stop=True).then_inc(s_QK_ready, 1)

            def body(i, L, Lp, A, B, l2, par=None):
                par = parity(i, par)
                for u in range(NU):
                    if body_is(i, -2) and u == 6:
                        vectors()
                        pe.wait_ge(s_w_sb, 1)
                    if body_is(i, -1) and u == 6:
                        pe.wait_ge(s_w_rest, 16 * 5)
                        weights_T(range(1, len(wbanks)))
                    if body_is(i, 0) and u == 0:
                        pe.wait_ge(s_w_sb, len(wbanks))
                    if L is not None:
                        scores(i, u, par)
                    if u == 6 and Lp == 0:
                        project(i, Lp, B, l2)
                    if u >= LT and L is not None:
                        turn(i, u - LT)
                    elif u < LT and Lp is not None:
                        turn(i - 1, u - LT + NU)
                    if u == 6 and Lp == 1:
                        project(i, Lp, B, l2)
                    if u >= LP and L is not None:
                        values(i, u - LP, par)
                    elif u < LP and Lp is not None:
                        values(i - 1, u - LP + NU, 1 - par)
                    if Lp is not None and u in (0, 4):
                        o_turn(i - 1, u // 4)
                    if Lp is not None and u in (2, 5):
                        o_back(i - 1, u // 4)
                    side(i, u, L, Lp, A, B, l2)

            schedule(pe, body)

        @block.scalar
        def _(act):
            A = nc.scalar.activation
            for r, v, k in ((BQ, bq, 1), (BK, bk, 1), (BV, bv, 1), (G1, g1, 1), (BE1, be1, 1), (G2, g2, 1)):
                act.dma_start(vec_rows[r:r + k], row(v)).then_inc(s_vec_rows, 16)
            act.wait_ge(s_ident, 2)
            A(table[:], ident[:, 0:1], ACT.Exp)
            act.wait_ge(s_vecs, 3)

            def exps(i, u):
                act.wait_ge(s_turned, NU * i + u + 1)
                if above_zero(NU * i + u + 1 - RP):
                    act.wait_ge(s_values, NU * i + u + 1 - RP)
                A(p_sb[:, u % RP], E_ps[u % 2][:, :], ACT.Exp).then_inc(s_exps, 1)

            def o_out(i, b):
                act.wait_ge(s_values, NU * i + UB * (b + 1))
                A(oT_aug[:], O_ps[b][:, 0:NT * VW], ACT.Copy).then_inc(s_o_out, 1)

            def a_out(i, b, L):
                act.wait_ge(s_o_back, GB * i + b + 1)
                bias = vec[:, BV1:BV1 + 1] if L else vec[:, BV:BV + 1]
                A(aT[:, b], O_ps[b][:, 0:128], ACT.Identity, bias=bias).then_inc(s_aT, 1)

            def v_out(i, par):
                if not above_zero(i - 1):
                    act.wait_ge(s_ones, 2 * (i + 1))
                act.wait_ge(s_V_ready, i + 1)
                if above_zero(NU * (i - 1)):
                    act.wait_ge(s_values, NU * (i - 1))
                A(v_aug[:, par, :, :, :, 0:HD].rearrange("p b t y d -> p (b t y) d"),
                  BANK["V"][:, 0:TG].rearrange("p (n d) -> p n d", d=HD), ACT.Copy).then_inc(s_v_aug, 1)

            def split_first(kind, grp, par, src, bias):
                act.wait_ge(s_QK_ready, grp + 1)
                if above_zero(grp - 1):
                    act.wait_ge(s_stack[kind][par], stacked(kind, grp - 2, par))
                A(parts[kind][:, par, 0], src, ACT.Identity, bias=bias).then_inc(s_first[kind], 1)

            def split_second(kind, grp, par):
                act.wait_ge(s_resid[kind], grp + 1)
                A(parts[kind][:, par, 1], resid[kind][:], ACT.Copy).then_inc(s_part2[kind], 1)

            def side(i, u, L, Lp, Ab, B, l2, par):
                if u == 0 and l2:
                    act.wait_ge(s_R2_ready, i - 1)
                    A(t2T[:], BANK["R2"][:, 0:TG], ACT.Identity, bias=col(vec, BE2), scale=col(vec, G2)).then_inc(s_R2_out, 1)
                if u == 0 and B == 0:
                    split_second("k", i + 1, 1 - par)
                    split_second("q", i + 1, 1 - par)
                if u == 1 and l2:
                    act.wait_ge(s_R3a_ready, i - 1)
                    for j in range(2):
                        A(hT[:, j], BANK["R3a"][:, j * TG:(j + 1) * TG], ACT.Relu, bias=col(vec, B1 + j)).then_inc(s_R3a_out, 1)
                if u == 2 and B == 1:
                    act.wait_ge(s_V_ready, i + 1)
                    act.wait_ge(s_c_kept, NG)
                    A(cT[:], cT_of(i + 1 - NG), ACT.Copy).then_inc(s_c_back, 1)
                if u == 4 and B is not None:
                    v_out(i + 1, 1 - par)
                if u == 5 and l2:
                    act.wait_ge(s_R5_ready, i - 1)
                    A(x3T_of(i - 2), BANK["R5"][:, 0:TG], ACT.Copy).then_inc(s_R5_out, 1)
                if u == 5 and Ab == 0:
                    act.wait_ge(s_P1_ready, i + 3)
                    if above_zero(i + 2):
                        act.wait_ge(s_c_kept, i + 2)
                    A(tT[:], BANK["P1"][:, 0:TG], ACT.Identity, bias=col(vec, BE1), scale=col(vec, G1)).then_inc(s_P1_out, 1)
                    A(cT[:], BANK["P1"][:, TG:2 * TG], ACT.Copy).then_inc(s_P1_out, 1)
                if u == qk_slot(Ab, l2) and Ab is not None:
                    split_first("k", i + 2, par, BANK["QK"][:, 0:TG], col(vec_p, BK1 if Ab else BK))
                    split_first("q", i + 2, par, BANK["QK"][:, TG:2 * TG], col(vec_p, BQ1 if Ab else BQ))
                if u == 7 and Ab == 0:
                    act.wait_ge(s_P1_out, 2 * (i + 3))
                    A(cT_of(i + 2), cT[:], ACT.Copy).then_inc(s_c_kept, 1)
                if u == (7 if l2 else 4) and Ab == 1:
                    split_second("k", i + 2, par)
                    split_second("q", i + 2, par)

            def body(i, L, Lp, Ab, B, l2, par=None):
                par = parity(i, par)
                for u in range(NU):
                    if body_is(i, -1) and u == 6:
                        for c in (1, 2):
                            act.wait_ge(s_w_T, c + 1)
                            A(W(4 * c, 4), wbanks[c][:, :], ACT.Copy).then_inc(s_w_sb, 1)
                    if u >= LT and L is not None:
                        exps(i, u - LT)
                    elif u < LT and Lp is not None:
                        exps(i - 1, u - LT + NU)
                    if Lp is not None and u == 3:
                        o_out(i - 1, 1)
                    if L is not None and u == 7:
                        o_out(i, 0)
                    if Lp is not None and u in (2, 5):
                        a_out(i - 1, u // 4, Lp)
                    side(i, u, L, Lp, Ab, B, l2, par)

            schedule(act, body)

        @block.vector
        def _(dve):
            V = nc.vector
            V.memset(q_st[:, 0], 0.0).then_inc(s_zeroed[0], 1)

            def first_weights():
                dve.wait_ge(s_w_T, 1)
                for n in (W_K, W_Q):
                    V.tensor_scalar(W(n).rearrange("p (d h) -> p d h", d=HD),
                                    wbanks[0][:, n * 128:(n + 1) * 128].rearrange("p (h d) -> p d h", d=HD),
                                    SCALE if n == W_Q else 1.0, None, ALU.mult)
                V.tensor_copy(W(2, 2), wbanks[0][:, 256:512]).then_inc(s_w_sb, 1)

            def vectors():
                dve.wait_ge(s_vec_rows, 16 * VECS_ACT)
                dve.wait_ge(s_vec_rows_pool, 16 * VECS_POOL)
                V.tensor_copy(vec_rows_p[:, :].rearrange("r (d h) -> r d h", d=HD),
                              vec_rows[:, :].rearrange("r (h d) -> r d h", d=HD)).then_inc(s_rows_p, 1)
                dve.wait_ge(s_vec_T, 1)
                V.tensor_copy(vec[:], O_ps[0][:, 0:NVEC])
                V.tensor_copy(vec_p[:], O_ps[0][:, 32:32 + NVEC]).then_inc(s_vecs, 1)
                dve.wait_ge(s_vecs, 1)
                for n in (BQ, BQ1):
                    V.tensor_scalar(col(vec_p, n), col(vec_p, n), SCALE, None, ALU.mult).then_inc(s_vecs, 1)

            def other_weights():
                dve.wait_ge(s_w_T, 4)
                V.tensor_copy(W(W_2 + NJ - 1), wbanks[3][:, 0:128])
                for n in (W_Q1, W_K1):
                    V.tensor_scalar(W(n).rearrange("p (d h) -> p d h", d=HD),
                                    wbanks[3][:, (n - 12) * 128:(n - 11) * 128].rearrange("p (h d) -> p d h", d=HD),
                                    SCALE if n == W_Q1 else 1.0, None, ALU.mult)
                V.tensor_copy(W(W_V1), wbanks[3][:, 384:512]).then_inc(s_w_sb, 1)
                dve.wait_ge(s_w_T, 5)
                V.tensor_copy(W(W_O1), wbanks[4][:, 0:128]).then_inc(s_w_sb, 1)

            def mask_bias(grp, b):
                dve.wait_ge(s_m_in[b], 16 * (grp + 1))
                V.tensor_scalar(mbias[:, b], m_in[:, b], -1.0, BIG, ALU.add, ALU.mult).then_inc(s_mbias[b], 1)

            def masked_max(i, u, L):
                b = u // UB
                dve.wait_ge(s_scores, NU * i + u + 1)
                if above_zero(NU * i + u + 1 - RT):
                    dve.wait_ge(s_turned, NU * i + u + 1 - RT)
                if L == 0 and u % UB == 0:
                    dve.wait_ge(s_mbias[b], i + 1)
                settled(dve, i)
                for j in range(UH):
                    t, s, m = t_sb[:, u % RT, j], S_ps[u % 2][:, j * S:(j + 1) * S], mx[:, u % RT, j:j + 1]
                    if L == 0:
                        last = V.tensor_tensor_reduce(t, s, mbias[:, b], 1.0, -3.4e38, ALU.add, ALU.max, m)
                    else:
                        last = V.tensor_scalar(t, s, 1.0, None, ALU.mult, ALU.max, accum_out=m)
                last.then_inc(s_masked, 1)

            def normalise(i, b):
                dve.wait_ge(s_o_turned, GB * i + b + 1)
                nv = O_ps[b][:, 0:NT * VW].rearrange("p (t w) -> p t w", w=VW)[:, :, 0:2 * OW].rearrange(
                    "p t (y e) -> p t y e", e=OW)
                rv = rden[:].rearrange("p (t y) -> p t y", y=2)
                V.reciprocal(rv, nv[:, :, :, HD]).then_inc(s_rden, 1)
                dve.wait_ge(s_rden, GB * i + b + 1)
                V.tensor_tensor(o_n[:, :, :].rearrange("p (t y) d -> p t y d", y=2), nv[:, :, :, 0:HD],
                                rv.unsqueeze(3).to_broadcast([128, NT, 2, HD]), ALU.mult).then_inc(s_o_n, 1)

            def norm_stats(k, src, n):
                for b in range(GB):
                    last = V.bn_stats(stats[k][:, b], src[:, b * D:(b + 1) * D])
                last.then_inc(s_ln[k], 1)
                dve.wait_ge(s_ln[k], 2 * n + 1)
                settled(dve, n)
                for b in range(GB):
                    last = V.bn_aggr(mv[k][:, b], stats[k][:, b])
                last.then_inc(s_ln[k], 1)

            def norm_apply(k, dst, src, n, done):
                dve.wait_ge(s_rstd[k], n + 1)
                for b in range(GB):
                    last = V.tensor_scalar(dst[:, b], src[:, b * D:(b + 1) * D], mv[k][:, b, 0:1], rstd[k][:, b:b + 1],
                                           ALU.subtract, ALU.mult)
                last.then_inc(done, 1)

            def norm_scale(n):
                dve.wait_ge(s_rep, 16 * NREP)
                dve.wait_ge(s_ln["b"], 2 * n + 2)
                settled(dve, n)
                for b in range(GB):
                    last = V.scalar_tensor_tensor(yg[:, b], x2[:, b * D:(b + 1) * D], mv["b"][:, b, 0:1], rep[:, R_GAM],
                                                  ALU.subtract, ALU.mult)
                last.then_inc(s_yg, 1)
                dve.wait_ge(s_yg, n + 1 - NG)
                if above_zero(16 * (n - NG)):
                    dve.wait_ge(s_stored, 16 * (n - NG))
                dve.wait_ge(s_rstd["b"], n + 1)
                settled(dve, n)
                for b in range(GB):
                    last = V.scalar_tensor_tensor(y_out[:, b], yg[:, b], rstd["b"][:, b:b + 1], rep[:, R_BET],
                                                  ALU.mult, ALU.add)
                last.then_inc(s_y_out, 1)

            def split_resid(kind, grp, par, src, bias):
                for k in "kq":
                    dve.wait_ge(s_first[k], grp + 1)
                V.scalar_tensor_tensor(resid[kind][:], src, bias, parts[kind][:, par, 0], ALU.add, ALU.subtract
                                       ).then_inc(s_resid[kind], 1)

            def split_third(kind, grp, par):
                dve.wait_ge(s_part2[kind], grp + 1)
                V.tensor_tensor(parts[kind][:, par, 2], resid[kind][:], parts[kind][:, par, 1], ALU.subtract).then_inc(s_part3[kind], 1)

            def side(i, u, L, Lp, A, B, l2, par):
                if L == 0 and u == 1:
                    mask_bias(i, 1)
                if B == 0 and u == 5:
                    mask_bias(i + 1, 0)
                if u == 1 and (B == 0 or B == 1 and l2):
                    split_third("k", i + 1, 1 - par)
                    split_third("q", i + 1, 1 - par)
                if u == 2 and l2:
                    dve.wait_ge(s_R3b_ready, i - 1)
                    for j in range(2):
                        V.tensor_scalar(hT[:, 2 + j], BANK["R3b"][:, j * TG:(j + 1) * TG], vec[:, B1 + 2 + j:B1 + 3 + j], 0.0,
                                        ALU.add, ALU.max).then_inc(s_R3b_out, 1)
                if u == 3 and A == 0:
                    dve.wait_ge(s_x_in, 16 * (i + 3))
                    norm_stats("a", flat(x_in), i + 2)
                if u == 4 and l2:
                    dve.wait_ge(s_R4_ready, i - 1)
                    dve.wait_ge(s_x2b, i - 1)
                    V.tensor_tensor(x3[:], BANK["R4"][:, 0:TG], x2b[:], ALU.add).then_inc(s_x3, 1)
                if u == 4 and A == 0:
                    if above_zero(i + 2):
                        dve.wait_ge(s_P1_ready, i + 2)
                    norm_apply("a", xn, flat(x_in), i + 2, s_xn)
                if u == 4 and B == 0:
                    dve.wait_ge(s_v_aug, i + 2)
                    dve.wait_ge(s_V_ready, i + 2)
                    dve.wait_ge(s_xb, i + 2)
                    V.tensor_tensor(xg_all[:, bass.ts(i + 1, TG)], BANK["V"][:, TG:2 * TG], xb[:], ALU.add).then_inc(s_xg, 1)
                if u == 6 and Lp is not None:
                    dve.wait_ge(s_OP_ready, i)
                    if Lp == 0:
                        if above_zero(i - 1):
                            dve.wait_ge(s_x2b, i - 1)
                        dve.wait_ge(s_xg, i)
                        res = xg_all[:, bass.ts(i - 1, TG)]
                    else:
                        dve.wait_ge(s_x2b, NG)
                        dve.wait_ge(s_x3b, NG)
                        res = x3b_all[:, bass.ts(i - 1 - NG, TG)]
                    V.tensor_tensor(x2[:], BANK["OP"][:, 0:TG], res, ALU.add).then_inc(s_OP_out, 1)
                    dve.wait_ge(s_OP_out, i)
                    norm_stats("b", x2, i - 1)
                if u == 7 and Lp == 0:
                    if above_zero(i - 1):
                        dve.wait_ge(s_R2_ready, i - 1)
                    norm_apply("b", xn2, x2, i - 1, s_xn2)
                if u == 7 and Lp == 1:
                    norm_scale(i - 1)
                if u == qk_slot(A, l2) + 1 and A is not None:
                    split_resid("k", i + 2, par, BANK["QK"][:, 0:TG], col(vec_p, BK1 if A else BK))
                    split_resid("q", i + 2, par, BANK["QK"][:, TG:2 * TG], col(vec_p, BQ1 if A else BQ))
                if A == 1 and (u == 5 and not l2 or u == 7 and body_is(i, NG + 1)):
                    split_third("k", i + 2, par)
                    split_third("q", i + 2, par)

            def body(i, L, Lp, A, B, l2, par=None):
                par = parity(i, par)
                for u in range(NU):
                    if body_is(i, -2) and u == 5:
                        first_weights()
                        vectors()
                    if body_is(i, -1) and u == 6:
                        V.memset(q_st[:, 1], 0.0).then_inc(s_zeroed[1], 1)
                        other_weights()
                    if L is not None:
                        masked_max(i, u, L)
                    if Lp is not None and u in (0, 4):
                        normalise(i - 1, u // 4)
                    side(i, u, L, Lp, A, B, l2, par)

            schedule(dve, body)

        @block.gpsimd
        def _(pool):
            G = nc.gpsimd
            G.memset(ident[:], 0.0).then_inc(s_ident, 1)
            pool.wait_ge(s_ident, 1)
            G.affine_select(out=ident[:], in_=ident[:], compare_op=ALU.not_equal, fill=1.0, base=0, pattern=[[-1, 128]],
                            channel_multiplier=1).then_inc(s_ident, 1)
            G.memset(expo[:], -0.5)
            for r, v, k in ((BE2, be2, 1), (B1, b1, NJ), (BQ1, bqkv1, 3)):
                pool.dma_start(vec_rows[r:r + k], row(v)).then_inc(s_vec_rows_pool, 16)
            grouped = lambda t: t.rearrange("p (b d) -> p b d", b=GB)

            def shift(i, u):
                pool.wait_ge(s_masked, NU * i + u + 1)
                t = t_sb[:, u % RT]
                G.tensor_tensor(t, t, mx[:, u % RT].unsqueeze(2).to_broadcast([128, UH, S]), ALU.subtract).then_inc(s_shifted, 1)

            def inverse_root(k, n):
                pool.wait_ge(s_ln[k], 2 * n + 2)
                settled(pool, n)
                G.tensor_scalar(ve[k][:], mv[k][:, :, 1], EPS, None, ALU.add).then_inc(s_ve[k], 1)
                pool.wait_ge(s_ve[k], n + 1)
                G.tensor_tensor(rstd[k][:], ve[k][:], expo[:], ALU.pow).then_inc(s_rstd[k], 1)

            def body(i, L, Lp, A, B, l2, par=None):
                for u in range(NU):
                    if body_is(i, -2) and u == 4:
                        G.memset(k_st[:, 0], 0.0).then_inc(s_zeroed[0], 1)
                    if body_is(i, -2) and u == 5:
                        pool.wait_ge(s_rep, 16 * NREP)
                        G.tensor_tensor(bias_og[:], rep[:, R_BO], rep[:, R_BG], ALU.add).then_inc(s_bias_og, 1)
                        pool.wait_ge(s_bias_og, 1)
                    if body_is(i, -1) and u == 0:
                        for b in range(2):
                            G.memset(v_aug[:, b], 0.0).then_inc(s_ones, 1)
                            pool.wait_ge(s_ones, 2 * b + 1)
                            G.memset(v_aug[:, b, :, :, :, HD], 1.0).then_inc(s_ones, 1)
                    if L is not None:
                        shift(i, u)
                    if u == 3 and A == 0:
                        inverse_root("a", i + 2)
                    if u == 5 and l2:
                        pool.wait_ge(s_x3, i - 1)
                        G.tensor_tensor(grouped(x3b_all[:, bass.ts(i - 2, TG)]), grouped(x3[:]), per_row(rep[:, R_BO1]),
                                        ALU.add).then_inc(s_x3b, 1)
                    if u == 5 and A == 0:
                        pool.wait_ge(s_x_in, 16 * (i + 3))
                        if above_zero(i + 2):
                            pool.wait_ge(s_xg, i + 2)
                        G.tensor_tensor(grouped(xb[:]), x_in[:, :, :], per_row(bias_og[:]), ALU.add).then_inc(s_xb, 1)
                    if body_is(i, -1) and u == 6:
                        G.memset(k_st[:, 1], 0.0).then_inc(s_zeroed[1], 1)
                    if u == 6 and Lp is not None:
                        inverse_root("b", i - 1)
                    if u == 7 and Lp == 0:
                        pool.wait_ge(s_OP_out, i)
                        if above_zero(i - 1):
                            pool.wait_ge(s_x3, i - 1)
                        G.tensor_tensor(grouped(x2b[:]), grouped(x2[:]), per_row(rep[:, R_B2]), ALU.add).then_inc(s_x2b, 1)

            schedule(pool, body)


_INS = ["x", "ctx_1024", "mask_BxSxS2_fk0", "L0_xattn_Wq", "L0_xattn_bq", "L0_xattn_Wk", "L0_xattn_bk", "L0_xattn_Wv",
        "L0_xattn_bv", "L0_xattn_Wo", "L0_xattn_bo", "L0_xattn_Wg", "L0_xattn_bg", "L0_xattn_W1", "L0_xattn_b1",
        "L0_xattn_W2", "L0_xattn_b2", "L0_xattn_g1", "L0_xattn_be1", "L0_xattn_g2", "L0_xattn_be2", "L1_xattn_W_qkv",
        "L1_xattn_b_qkv", "L1_xattn_W_o", "L1_xattn_b_o", "L1_xattn_ln_gamma", "L1_xattn_ln_beta"]
_OUTS = [((NB, S, D), "float32")]


def kernel(**inputs):
    import numpy as _np
    import concourse.bacc as _bacc
    from concourse import mybir as _mybir
    from concourse.bass_utils import run_bass_kernel_spmd as _run

    nc = _bacc.Bacc("TRN2", target_bir_lowering=False, num_devices=1)
    arrays, args = {}, []
    for name in _INS:
        a = _np.ascontiguousarray(inputs[name])
        arrays[f"in_{name}_dram"] = a
        args.append(nc.dram_tensor(f"in_{name}_dram", a.shape, _mybir.dt.from_np(a.dtype), kind="ExternalInput").ap())
    for n, (shape, dtype) in enumerate(_OUTS):
        dt = _mybir.dt.from_np(_np.dtype(dtype))
        args.append(nc.dram_tensor(f"out_{n}_dram", shape, dt, kind="ExternalOutput").ap())
    build(nc, *args)
    r = _run(nc, [arrays], core_ids=[0])
    return tuple(r.results[0][f"out_{n}_dram"] for n in range(len(_OUTS)))[0]
```
